# Optimizing a Trainium2 kernel written in Bass

```python
import numpy as np
import jax
import jax.numpy as jnp

def _softmax(x, axis=-1):
    return jax.nn.softmax(x, axis=axis)

def _gelu(x):
    return jax.nn.gelu(x, approximate=True)

def _silu(x):
    return jax.nn.silu(x)

def _sigmoid(x):
    return jax.nn.sigmoid(x)

def _layernorm(x, axis=-1, eps=1e-05):
    m = jnp.mean(x, axis=axis, keepdims=True)
    v = jnp.var(x, axis=axis, keepdims=True)
    return (x - m) / jnp.sqrt(v + eps)

def _scatter_add(tgt, idx, src, axis=0):
    return tgt.at[idx].add(src)

def _segment_sum(src, seg, n):
    return jax.ops.segment_sum(src, seg, n)
kernel_name = 'mk_seq_preln_d1_jaxref_r4_321969'

def setup_inputs(seed: int=0):
    np.random.seed(seed)
    _w = jnp.asarray

    def _L0_attn_setup():
        import jax, jax.numpy as jnp
        import numpy as np
        B, S, DM = (2, 512, 512)
        H, KVH, HD = (16, 4, 128)
        REP = H // KVH
        ROPE_BASE = 10000.0
        EPS = 1e-06

        def _rope_tables(seq_len, dim):
            inv_freq = 1.0 / ROPE_BASE ** (jnp.arange(0, dim, 2, dtype=jnp.float32) / dim)
            t = jnp.arange(seq_len, dtype=jnp.float32)
            freqs = jnp.outer(t, inv_freq)
            emb = jnp.concatenate([freqs, freqs], -1)
            return (jnp.cos(emb), jnp.sin(emb))

        def _rotate_half(x):
            d = x.shape[-1] // 2
            return jnp.concatenate([-x[..., d:], x[..., :d]], axis=-1)
        key = jax.random.key(seed)
        k0, k1, k2, k3, k4 = jax.random.split(key, 5)
        w = lambda k, o, i: jax.random.normal(k, (o, i), jnp.float32) * (1.0 / np.sqrt(i))
        return {'x': jax.random.normal(k0, (B, S, DM), jnp.float32), 'Wq': w(k1, H * HD, DM), 'Wk': w(k2, KVH * HD, DM), 'Wv': w(k3, KVH * HD, DM), 'Wo': w(k4, DM, H * HD)}
    _L0_attn_in = _L0_attn_setup()

    def _L0_ffn_setup():
        import jax, jax.numpy as jnp
        import numpy as np
        B, S, H = (2, 256, 512)
        I = 256
        E = 32
        Z = 32
        K = 8
        SCALE = 1.5
        CAP = 256
        EPS = 1e-20

        def _moe_forward(x, w_cls, bias, w_gate_up, w_down):
            T = x.shape[0] * x.shape[1]
            xf = x.reshape(T, H)
            logits = xf.astype(jnp.float32) @ w_cls.T
            scores = jax.nn.softmax(logits, axis=-1)
            _, topk_idx = jax.lax.top_k(scores + bias[None, :], K)
            w = jnp.take_along_axis(scores, topk_idx, axis=-1)
            w = w / (w.sum(-1, keepdims=True) + EPS) * SCALE
            routed = topk_idx < E
            w_r = jnp.where(routed, w, 0.0)
            w_z = jnp.where(routed, 0.0, w)
            N = T * K
            flat_ids = jnp.where(routed, topk_idx, E).reshape(-1)
            x_exp = jnp.repeat(xf, K, axis=0)
            order = jnp.argsort(flat_ids)
            ids_s = flat_ids[order]
            counts = jax.ops.segment_sum(jnp.ones(N, jnp.int32), flat_ids, num_segments=E + 1)
            starts = jnp.cumsum(counts) - counts
            pos = jnp.arange(N) - starts[ids_s]
            buf = jnp.zeros((E, CAP, H), xf.dtype).at[ids_s, pos].set(x_exp[order], mode='drop')
            gu = jnp.einsum('ech,ehf->ecf', buf, w_gate_up)
            g, u = jnp.split(gu, 2, axis=-1)
            act = jax.nn.silu(g) * u
            y = jnp.einsum('eci,eih->ech', act, w_down)
            valid = (ids_s < E) & (pos < CAP)
            y_tok = jnp.where(valid[:, None], y[jnp.clip(ids_s, 0, E - 1), jnp.clip(pos, 0, CAP - 1)], 0.0)
            y_exp = jnp.zeros((N, H), xf.dtype).at[order].set(y_tok).reshape(T, K, H)
            routed_out = jnp.einsum('tk,tkh->th', w_r, y_exp)
            out = routed_out * (1.0 + w_z.sum(-1, keepdims=True))
            return out.reshape(x.shape)
        key = jax.random.key(seed)
        ks = jax.random.split(key, 5)
        x = jax.random.normal(ks[0], (B, S, H), jnp.float32)
        w_cls = jax.random.normal(ks[1], (E + Z, H), jnp.float32) / np.float32(np.sqrt(H))
        bias = jax.random.normal(ks[2], (E + Z,), jnp.float32) * 0.02
        w_gate_up = jax.random.normal(ks[3], (E, H, 2 * I), jnp.float32) * 0.02
        w_down = jax.random.normal(ks[4], (E, I, H), jnp.float32) * 0.02
        return {'x': x, 'w_cls': w_cls, 'bias': bias, 'w_gate_up': w_gate_up, 'w_down': w_down}
    _L0_ffn_in = _L0_ffn_setup()
    _d = {'L0_attn_x': _L0_attn_in['x'], 'L0_attn_Wq': _L0_attn_in['Wq'], 'L0_attn_Wk': _L0_attn_in['Wk'], 'L0_attn_Wv': _L0_attn_in['Wv'], 'L0_attn_Wo': _L0_attn_in['Wo'], 'L0_ffn_w_cls': _L0_ffn_in['w_cls'], 'L0_ffn_bias': _L0_ffn_in['bias'], 'L0_ffn_w_gate_up': _L0_ffn_in['w_gate_up'], 'L0_ffn_w_down': _L0_ffn_in['w_down']}
    _x0 = _d['L0_attn_x']
    _d['L0_attn_x'] = jax.random.normal(jax.random.fold_in(jax.random.key(seed), 1), (1, 2048, 512), dtype=_x0.dtype)
    del _x0
    return _d

def reference(L0_attn_x, L0_attn_Wq, L0_attn_Wk, L0_attn_Wv, L0_attn_Wo, L0_ffn_w_cls, L0_ffn_bias, L0_ffn_w_gate_up, L0_ffn_w_down):

    def _L0_attn_ref(x, Wq, Wk, Wv, Wo):
        import jax, jax.numpy as jnp
        import numpy as np
        B, S, DM = (2, 512, 512)
        H, KVH, HD = (16, 4, 128)
        REP = H // KVH
        ROPE_BASE = 10000.0
        EPS = 1e-06

        def _rope_tables(seq_len, dim):
            inv_freq = 1.0 / ROPE_BASE ** (jnp.arange(0, dim, 2, dtype=jnp.float32) / dim)
            t = jnp.arange(seq_len, dtype=jnp.float32)
            freqs = jnp.outer(t, inv_freq)
            emb = jnp.concatenate([freqs, freqs], -1)
            return (jnp.cos(emb), jnp.sin(emb))

        def _rotate_half(x):
            d = x.shape[-1] // 2
            return jnp.concatenate([-x[..., d:], x[..., :d]], axis=-1)
        bsz, seq_len, _ = x.shape
        q = (x @ Wq.T).reshape(bsz, seq_len, H, HD).transpose(0, 2, 1, 3)
        k = (x @ Wk.T).reshape(bsz, seq_len, KVH, HD).transpose(0, 2, 1, 3)
        v = (x @ Wv.T).reshape(bsz, seq_len, KVH, HD).transpose(0, 2, 1, 3)
        cos, sin = _rope_tables(seq_len, HD)
        cos, sin = (cos[None, None], sin[None, None])
        q = q * cos + _rotate_half(q) * sin
        k = k * cos + _rotate_half(k) * sin
        k = jnp.repeat(k, REP, axis=1)
        v = jnp.repeat(v, REP, axis=1)
        qf = jax.nn.elu(q) + 1.0
        kf = jax.nn.elu(k) + 1.0
        qf_t = qf.transpose(2, 0, 1, 3)
        kf_t = kf.transpose(2, 0, 1, 3)
        v_t = v.transpose(2, 0, 1, 3)

        def step(carry, inp):
            state, z = carry
            q_s, k_s, v_s = inp
            state = state + k_s[..., :, None] * v_s[..., None, :]
            z = z + k_s
            num = jnp.einsum('bhe,bhed->bhd', q_s, state)
            den = jnp.einsum('bhe,bhe->bh', q_s, z)[..., None] + EPS
            return ((state, z), num / den)
        init = (jnp.zeros((bsz, H, HD, HD), x.dtype), jnp.zeros((bsz, H, HD), x.dtype))
        _, out = jax.lax.scan(step, init, (qf_t, kf_t, v_t))
        out = out.transpose(1, 0, 2, 3).reshape(bsz, seq_len, H * HD)
        return out @ Wo.T

    def _L0_ffn_ref(x, w_cls, bias, w_gate_up, w_down):
        import jax, jax.numpy as jnp
        import numpy as np
        B, S, H = (2, 256, 512)
        I = 256
        E = 32
        Z = 32
        K = 8
        SCALE = 1.5
        CAP = 256
        EPS = 1e-20

        def _moe_forward(x, w_cls, bias, w_gate_up, w_down):
            T = x.shape[0] * x.shape[1]
            xf = x.reshape(T, H)
            logits = xf.astype(jnp.float32) @ w_cls.T
            scores = jax.nn.softmax(logits, axis=-1)
            _, topk_idx = jax.lax.top_k(scores + bias[None, :], K)
            w = jnp.take_along_axis(scores, topk_idx, axis=-1)
            w = w / (w.sum(-1, keepdims=True) + EPS) * SCALE
            routed = topk_idx < E
            w_r = jnp.where(routed, w, 0.0)
            w_z = jnp.where(routed, 0.0, w)
            N = T * K
            flat_ids = jnp.where(routed, topk_idx, E).reshape(-1)
            x_exp = jnp.repeat(xf, K, axis=0)
            order = jnp.argsort(flat_ids)
            ids_s = flat_ids[order]
            counts = jax.ops.segment_sum(jnp.ones(N, jnp.int32), flat_ids, num_segments=E + 1)
            starts = jnp.cumsum(counts) - counts
            pos = jnp.arange(N) - starts[ids_s]
            buf = jnp.zeros((E, CAP, H), xf.dtype).at[ids_s, pos].set(x_exp[order], mode='drop')
            gu = jnp.einsum('ech,ehf->ecf', buf, w_gate_up)
            g, u = jnp.split(gu, 2, axis=-1)
            act = jax.nn.silu(g) * u
            y = jnp.einsum('eci,eih->ech', act, w_down)
            valid = (ids_s < E) & (pos < CAP)
            y_tok = jnp.where(valid[:, None], y[jnp.clip(ids_s, 0, E - 1), jnp.clip(pos, 0, CAP - 1)], 0.0)
            y_exp = jnp.zeros((N, H), xf.dtype).at[order].set(y_tok).reshape(T, K, H)
            routed_out = jnp.einsum('tk,tkh->th', w_r, y_exp)
            out = routed_out * (1.0 + w_z.sum(-1, keepdims=True))
            return out.reshape(x.shape)
        return _moe_forward(x, w_cls, bias, w_gate_up, w_down)
    x = L0_attn_x
    x = x + _L0_attn_ref(_layernorm(x, axis=-1), L0_attn_Wq, L0_attn_Wk, L0_attn_Wv, L0_attn_Wo)
    x = x + _L0_ffn_ref(_layernorm(x, axis=-1), L0_ffn_w_cls, L0_ffn_bias, L0_ffn_w_gate_up, L0_ffn_w_down)
    return x

_drawn_inputs = setup_inputs


def setup_inputs(seed=0):
    import zlib

    import numpy as np

    out = dict(_drawn_inputs(seed))
    spreads = {}
    factors = {'L0_attn_Wq': 44.5,
     'L0_attn_Wk': 34.011,
     'L0_ffn_bias': 14.933,
     'L0_ffn_w_cls': 3.275,
     'L0_ffn_w_gate_up': 3.015,
     'L0_ffn_w_down': 3.021}
    for name, (base, spread) in spreads.items():
        noise = np.random.default_rng([zlib.crc32(name.encode()), seed]).standard_normal(out[name].shape)
        drawn = base * np.exp(spread * noise) if base else spread * noise
        out[name] = jnp.asarray(drawn.astype(out[name].dtype))
    for name, factor in factors.items():
        out[name] = (out[name] * factor).astype(out[name].dtype)
    return out
```

```python
from contextlib import ExitStack

import concourse.bass as bass
from concourse import mybir

P = 128
D = 512
T = 2048
NC = T // P
NH = 16
KV = 4
NG = NC * KV
NE = 32
E2 = 64
CW = 282

F32 = mybir.dt.float32
F32R = mybir.dt.float32r
I32 = mybir.dt.int32
U32 = mybir.dt.uint32
ALU = mybir.AluOpType
ACT = mybir.ActivationFunctionType
AX = mybir.AxisListType.X


class Events:

    def __init__(self, nc, ctx):
        self.nc, self.ctx, self.sems, self.seen = nc, ctx, {}, {}
        self.done, self.most = {}, {}

    def sem(self, kind):
        if kind not in self.sems:
            self.sems[kind] = self.ctx.enter_context(self.nc.semaphore("e_" + kind))
        return self.sems[kind]

    def did(self, ins, kind, by=1):
        ins.then_inc(self.sem(kind), by)
        self.done[kind] = self.done.get(kind, 0) + 1

    def wait(self, eng, kind, n, by=1):
        if n < 0:
            return
        key = (id(eng), kind)
        if self.seen.get(key, -1) < n:
            self.seen[key] = n
            self.most[kind] = max(self.most.get(kind, 0), n)
            eng.wait_ge(self.sem(kind), (n + 1) * by)

    def check(self):
        short = {k: (n, self.done.get(k, 0)) for k, n in self.most.items() if n >= self.done.get(k, 0)}
        assert not short, short


def attention(nc, ev, x, wq, wk, wv, tabs, consts, oT):
    with ExitStack() as ctx:
        def sb(name, shape, dt=F32):
            return ctx.enter_context(nc.sbuf_tensor("a_" + name, shape, dt))

        def ps(name):
            return ctx.enter_context(nc.psum_tensor("a_" + name, [P, 512], F32))

        w_h = sb("w_h", [P, 24, 512], F32R)
        w_l = sb("w_l", [P, 24, 512], F32R)
        xin = sb("xin", [P, 2, D])
        xn = sb("xn", [P, D])
        xT_h = sb("xT_h", [P, 2, 4, P], F32R)
        xT_l = sb("xT_l", [P, 2, 4, P], F32R)
        tab = sb("tab", [P, 2, 2, P])
        t1 = sb("t1", [P, 2, 512])
        t2 = sb("t2", [P, 2, 512])
        e = sb("e", [P, 2, 512])
        fK = sb("fK", [P, 512])
        fQ = sb("fQ", [P, 3, 512])
        m = sb("m", [P, 512])
        K_h = sb("K_h", [P, 512], F32R)
        K_l = sb("K_l", [P, 512], F32R)
        V_h = sb("V_h", [P, 2, 512], F32R)
        V_l = sb("V_l", [P, 2, 512], F32R)
        KT_h = sb("KT_h", [P, 2, 512], F32R)
        KT_l = sb("KT_l", [P, 2, 512], F32R)
        QT_h = sb("QT_h", [P, 2, 512], F32R)
        QT_l = sb("QT_l", [P, 2, 512], F32R)
        z = sb("z", [P, 512])
        z_h = sb("z_h", [P, 512], F32R)
        z_l = sb("z_l", [P, 512], F32R)
        A = sb("A", [P, 2, 512])
        A_h = sb("A_h", [P, 2, 512], F32R)
        A_l = sb("A_l", [P, 2, 512], F32R)
        o = sb("o", [P, 2, 512])
        S = sb("S", [P, 512])
        S_h = sb("S_h", [P, 2, 512], F32R)
        S_l = sb("S_l", [P, 2, 512], F32R)
        cst = sb("cst", [P, 3, P])
        tri_r = sb("tri_r", [P, P], F32R)
        last_r = sb("last_r", [P, P], F32R)
        st = sb("st", [P, 2, 6])
        mv = sb("mv", [P, 2, 2])
        vr = sb("vr", [P, 2, 2])
        neg = sb("neg", [P, 1])
        den = sb("den", [P, 2, 4])

        PQ = [ps("PQ0"), ps("PQ1")]
        PT = [ps("PT0"), ps("PT1")]
        PX, PS, PO, PM = ps("PX"), ps("PS"), ps("PO"), ps("PM")

        ident = cst[:, 0, :]
        tri = cst[:, 1, :]

        def f(ap):
            return ap.bitcast(F32)

        def heads(ap):
            return ap.rearrange("p (h d) -> p h d", h=4)

        def spread(ap):
            return ap.unsqueeze(1).broadcast_to([P, 4, ap.shape[-1]])

        def unit_k(c):
            return 6 * c

        def unit_v(c):
            return 6 * c + 1

        def unit_q(n):
            return 6 * (n // 4) + 2 + n % 4

        def rot_k(c):
            return 5 * c

        def rot_q(n):
            return 5 * (n // 4) + 1 + n % 4

        def plan():
            ops = []
            for n in range(NG + 5):
                c, g = divmod(n, 4)
                if g == 0 and c < NC:
                    ops += [("PK", c), ("PV", c)]
                if n < NG:
                    ops.append(("P", n))
                if 0 <= n - 5 < NG:
                    ops.append(("O", n - 5))
                if g == 0 and 1 <= c < NC:
                    ops.append(("U", c - 1))
                if g == 1 and c < NC:
                    ops += [("TK", c), ("ZC", c)]
                if 0 <= n - 3 < NG:
                    ops.append(("T", n - 3))
                if g == 2 and c + 1 < NC:
                    ops.append(("XT", c + 1))
                if 0 <= n - 4 < NG:
                    ops.append(("S", n - 4))
            return ops

        order = plan()
        turns = [op for op in order if op[0] in ("TK", "T")]
        turn = {op: j for j, op in enumerate(turns)}

        def piece(i):
            j, k = divmod(i, 4)
            rows = slice(k * P, (k + 1) * P)
            if j == 0:
                return wk[rows, :]
            if j == 1:
                return wv[rows, :]
            return wq[rows, (j - 2) * 512:(j - 1) * 512]

        def stage(i):
            return (A, o)[i % 4 // 2][:, i % 2, :]

        with nc.Block() as block:
            @block.sync
            def _(eng):
                def load_x(c):
                    ev.wait(eng, "xn", c - 2)
                    ev.did(eng.dma_start(xin[:, c % 2, :], x[c * P:(c + 1) * P, :]), f"x{c % 2}", 16)

                def load_tab(c):
                    if c >= 2:
                        ev.wait(eng, "pqfree", unit_q(4 * (c - 2) + 3))
                    ev.did(eng.dma_start(tab[:, c % 2, :, :], tabs[c]), f"tab{c % 2}", 16)

                load_x(0)
                ev.did(eng.dma_start(cst[:, :, :], consts), "cst", 16)
                for i in range(4):
                    ev.did(eng.dma_start(stage(i), piece(i)), f"st{i % 4}", 16)
                load_tab(0)
                load_x(1)
                load_tab(1)
                for i in range(4, 24):
                    ev.wait(eng, "wl", i - 4)
                    ev.did(eng.dma_start(stage(i), piece(i)), f"st{i % 4}", 16)
                for n in range(NG + 5):
                    c, g = divmod(n, 4)
                    if g == 0 and 1 <= c < NC - 1:
                        load_tab(c + 1)
                    if g == 2 and c + 2 < NC:
                        load_x(c + 2)
                    if n >= 5:
                        i = n - 5
                        ev.wait(eng, "o", i)
                        ev.did(eng.dma_start(oT[i // 4, :, 4 * (i % 4):4 * (i % 4) + 4, :],
                                             heads(o[:, i % 2, :])), f"oT{i % 2}", 16)
                for b in range(2):
                    ev.wait(eng, f"oT{b}", NG // 2 - 1, 16)

            @block.tensor
            def _(eng):
                def project(u, c, i):
                    ev.wait(eng, "pqfree", u - 2)
                    ev.wait(eng, "xTl", c)
                    ev.wait(eng, "wl", 4 * i + 3)
                    bank = PQ[u % 2]
                    xh, xl = xT_h[:, c % 2], xT_l[:, c % 2]
                    last = None
                    steps = [(xh, w_h), (xh, w_l), (xl, w_h)]
                    for s, (a, w) in enumerate(steps):
                        for k in range(4):
                            last = eng.matmul(bank[:, :], a[:, k, :], w[:, 4 * i + k, :],
                                              start=s == 0 and k == 0, stop=s == 2 and k == 3)
                    ev.did(last, "pq")

                def op_PK(c):
                    project(unit_k(c), c, 0)

                def op_PV(c):
                    project(unit_v(c), c, 1)

                def op_P(n):
                    project(unit_q(n), n // 4, 2 + n % 4)

                def op_XT(c):
                    ev.wait(eng, "cst", 0, 16)
                    ev.wait(eng, "xn", c)
                    ev.wait(eng, "xTl", c - 1)
                    for k in range(4):
                        last = eng.transpose(PX[:, k * P:(k + 1) * P], xn[:, k * P:(k + 1) * P], ident)
                    ev.did(last, "xt")

                def turned(src, j):
                    ev.wait(eng, "ptfree", j - 2)
                    for k in range(4):
                        last = eng.transpose(PT[j % 2][:, k * P:(k + 1) * P], src[:, k * P:(k + 1) * P], ident)
                    ev.did(last, "pt")

                def op_TK(c):
                    ev.wait(eng, "f", rot_k(c))
                    turned(fK[:, :], turn[("TK", c)])

                def op_T(n):
                    ev.wait(eng, "fs", n)
                    turned(fQ[:, n % 3, :], turn[("T", n)])

                def op_ZC(c):
                    ev.wait(eng, "trr", 0)
                    ev.wait(eng, "Kl", c)
                    ev.wait(eng, "S", c - 1)
                    eng.matmul(PM[:, :], tri_r[:, :], K_h[:, :], start=True, stop=False)
                    last = eng.matmul(PM[:, :], tri_r[:, :], K_l[:, :], start=False, stop=c == 0)
                    if c > 0:
                        ev.wait(eng, "zl", c - 1)
                        eng.matmul(PM[:, :], last_r[:, :], z_h[:, :], start=False, stop=False)
                        last = eng.matmul(PM[:, :], last_r[:, :], z_l[:, :], start=False, stop=True)
                    ev.did(last, "zc")

                def op_S(n):
                    c, g = divmod(n, 4)
                    ev.wait(eng, "ptfree", max(turn[("T", n)], turn[("TK", c)]))
                    ev.wait(eng, "A", n - 1)
                    kh, kl = (a[:, c % 2, g * P:(g + 1) * P] for a in (KT_h, KT_l))
                    qh, ql = QT_h[:, n % 2, :], QT_l[:, n % 2, :]
                    eng.matmul(PS[:, :], kh, qh, start=True, stop=False)
                    eng.matmul(PS[:, :], kh, ql, start=False, stop=False)
                    ev.did(eng.matmul(PS[:, :], kl, qh, start=False, stop=True), "sc")

                def op_O(n):
                    c, g = divmod(n, 4)
                    ev.wait(eng, "o", n - 1)
                    cols = slice(g * P, (g + 1) * P)
                    if c > 0:
                        ev.wait(eng, "Sl", c - 1)
                        sh, sl = S_h[:, c % 2, cols], S_l[:, c % 2, cols]
                        qh, ql = QT_h[:, n % 2, :], QT_l[:, n % 2, :]
                        eng.matmul(PO[:, :], sh, qh, start=True, stop=False)
                        eng.matmul(PO[:, :], sh, ql, start=False, stop=False)
                        eng.matmul(PO[:, :], sl, qh, start=False, stop=False)
                    ev.wait(eng, "pqfree", unit_v(c))
                    ev.wait(eng, "Al", n)
                    vh, vl = V_h[:, c % 2, cols], V_l[:, c % 2, cols]
                    ah, al = A_h[:, n % 2, :], A_l[:, n % 2, :]
                    eng.matmul(PO[:, :], vh, ah, start=c == 0, stop=False)
                    eng.matmul(PO[:, :], vh, al, start=False, stop=False)
                    ev.did(eng.matmul(PO[:, :], vl, ah, start=False, stop=True), "out")

                def op_U(c):
                    ev.wait(eng, "zl", c)
                    ev.wait(eng, "z", c)
                    ev.wait(eng, "pqfree", unit_v(c))
                    for g in range(4):
                        cols = slice(g * P, (g + 1) * P)
                        steps = [(K_h, V_h), (K_h, V_l), (K_l, V_h)]
                        for s, (a, b) in enumerate(steps):
                            last = eng.matmul(PM[:, cols], a[:, cols], b[:, c % 2, cols],
                                              start=s == 0, stop=s == 2)
                    ev.did(last, "u")

                ops = {"PK": op_PK, "PV": op_PV, "P": op_P, "XT": op_XT, "TK": op_TK, "T": op_T,
                       "ZC": op_ZC, "S": op_S, "O": op_O, "U": op_U}
                op_XT(0)
                for kind, i in order:
                    ops[kind](i)

            @block.vector
            def _(eng):
                ev.did(eng.memset(neg[:, :], -0.5), "neg")
                ev.wait(eng, "cst", 0, 16)
                eng.tensor_copy(tri_r[:, :], tri)
                ev.did(eng.tensor_copy(last_r[:, :], cst[:, 2, :]), "trr")

                def stats(c):
                    ev.wait(eng, f"x{c % 2}", c // 2, 16)
                    ev.did(eng.bn_stats(st[:, c % 2, :], xin[:, c % 2, :]), "bn")
                    ev.wait(eng, "bn", c)
                    ev.wait(eng, "xn", c - 2)
                    ev.did(eng.bn_aggr(mv[:, c % 2, :], st[:, c % 2, :]), "mv")

                def normal(c):
                    ev.wait(eng, "rstd", c)
                    ev.wait(eng, "mv", c)
                    ev.wait(eng, "xt", c - 1)
                    ev.did(eng.tensor_scalar(xn[:, :], xin[:, c % 2, :], mv[:, c % 2, 0:1], vr[:, c % 2, 1:2],
                                             ALU.subtract, ALU.mult), "xn")

                def xT_low(c):
                    ev.wait(eng, "xTh", c)
                    ev.did(eng.tensor_tensor(xT_l[:, c % 2, :, :].rearrange("p k t -> p (k t)"), PX[:, :],
                                             f(xT_h[:, c % 2, :, :]).rearrange("p k t -> p (k t)"),
                                             ALU.subtract), "xTl")

                def weight_low(i):
                    ev.wait(eng, "wh", i)
                    ev.did(eng.tensor_tensor(w_l[:, i, :], stage(i), f(w_h[:, i, :]), ALU.subtract), "wl")

                def rotate(u, r, c):
                    ev.wait(eng, "pq", u)
                    ev.wait(eng, f"tab{c % 2}", c // 2, 16)
                    ev.wait(eng, "f", r - 2)
                    q = heads(PQ[u % 2][:, :])
                    a, b = heads(t1[:, r % 2, :]), heads(t2[:, r % 2, :])
                    sn = tab[:, c % 2, 1, :]
                    eng.tensor_tensor(a, q, spread(tab[:, c % 2, 0, :]), ALU.mult)
                    eng.tensor_tensor(b[:, :, 0:64], q[:, :, 64:128], spread(sn[:, 0:64]), ALU.mult)
                    ev.did(eng.tensor_tensor(b[:, :, 64:128], q[:, :, 0:64], spread(sn[:, 64:128]), ALU.mult), "pqfree")

                def feature(r, out):
                    ev.wait(eng, "e", r)
                    ev.did(eng.scalar_tensor_tensor(out=out, in0=t1[:, r % 2, :], scalar=1.0, in1=e[:, r % 2, :],
                                                    op0=ALU.add, op1=ALU.max), "f")

                def feature_k(c):
                    ev.wait(eng, "Kl", c - 1)
                    ev.wait(eng, "Kh", c - 1)
                    if c >= 1:
                        ev.wait(eng, "pt", turn[("TK", c - 1)])
                    feature(rot_k(c), fK[:, :])

                def feature_q(n):
                    if n >= 3:
                        ev.wait(eng, "pt", turn[("T", n - 3)])
                    feature(rot_q(n), fQ[:, n % 3, :])

                def v_low(c):
                    if c >= 2:
                        ev.wait(eng, "out", 4 * (c - 2) + 3)
                        ev.wait(eng, "u", c - 2)
                    ev.wait(eng, "Vh", c)
                    ev.did(eng.tensor_tensor(V_l[:, c % 2, :], PQ[unit_v(c) % 2][:, :], f(V_h[:, c % 2, :]),
                                             ALU.subtract), "pqfree")

                def z_low(c):
                    ev.wait(eng, "z", c)
                    ev.did(eng.tensor_tensor(z_l[:, :], PM[:, :], f(z_h[:, :]), ALU.subtract), "zl")

                def reduce(n):
                    ev.wait(eng, "m", n)
                    ev.wait(eng, "fs", n - 2)
                    d = den[:, n % 2, :]
                    ev.did(eng.tensor_reduce(d, heads(m[:, :]), axis=AX, op=ALU.add), "den")
                    ev.wait(eng, "den", n)
                    ev.did(eng.tensor_scalar_add(d, d, 1e-6), "den1")
                    ev.wait(eng, "den1", n)
                    ev.did(eng.reciprocal(d, d), "rden")

                def turn_low(j):
                    kind, i = turns[j]
                    h, l = (KT_h, KT_l) if kind == "TK" else (QT_h, QT_l)
                    if kind == "TK":
                        ev.wait(eng, "sc", 4 * (i - 2) + 3)
                    else:
                        ev.wait(eng, "out", i - 2)
                    ev.wait(eng, "th", j)
                    ev.did(eng.tensor_tensor(l[:, i % 2, :], PT[j % 2][:, :], f(h[:, i % 2, :]), ALU.subtract),
                           "ptfree")

                def masked(n):
                    ev.wait(eng, "sc", n)
                    ev.wait(eng, "Al", n - 2)
                    ev.wait(eng, "Ah", n - 2)
                    ev.did(eng.tensor_tensor(heads(A[:, n % 2, :]), heads(PS[:, :]), spread(tri), ALU.mult), "A")

                def state(c):
                    ev.wait(eng, "u", c)
                    if c == 0:
                        ins = eng.tensor_copy(S[:, :], PM[:, :])
                    else:
                        ev.wait(eng, "Sh", c - 1)
                        ev.wait(eng, "Sl", c - 1)
                        ins = eng.tensor_tensor(S[:, :], PM[:, :], S[:, :], ALU.add)
                    ev.did(ins, "S")

                stats(0)
                normal(0)
                weight_low(0)
                xT_low(0)
                for i in range(1, 8):
                    weight_low(i)
                for n in range(NG + 5):
                    c, g = divmod(n, 4)
                    if g == 0 and c < NC:
                        rotate(unit_k(c), rot_k(c), c)
                        if c > 0:
                            feature_q(n - 1)
                        v_low(c)
                    if c == 0:
                        for i in range(8 + 4 * g, 12 + 4 * g):
                            weight_low(i)
                    if n < NG:
                        rotate(unit_q(n), rot_q(n), c)
                    if g == 0 and c < NC:
                        feature_k(c)
                    if g == 0 and 1 <= c < NC:
                        state(c - 1)
                    if g != 0 and n - 1 < NG or n == NG:
                        feature_q(n - 1)
                    if g == 0 and c + 1 < NC:
                        stats(c + 1)
                    if g == 1 and c < NC:
                        turn_low(turn[("TK", c)])
                        z_low(c)
                    if 0 <= n - 3 < NG:
                        turn_low(turn[("T", n - 3)])
                    if g == 1 and c + 1 < NC:
                        normal(c + 1)
                    if 0 <= n - 2 < NG:
                        reduce(n - 2)
                    if g == 2 and c + 1 < NC:
                        xT_low(c + 1)
                    if 0 <= n - 4 < NG:
                        masked(n - 4)

            @block.scalar
            def _(eng):
                def copy(out, in_, kind):
                    ev.did(eng.activation(out, in_, ACT.Copy), kind)

                def weight_high(i):
                    ev.wait(eng, f"st{i % 4}", i // 4, 16)
                    copy(w_h[:, i, :], stage(i), "wh")

                def xT_high(c):
                    ev.wait(eng, "xt", c)
                    if c >= 2:
                        ev.wait(eng, "pq", unit_q(4 * (c - 2) + 3))
                    copy(xT_h[:, c % 2, :, :].rearrange("p k t -> p (k t)"), PX[:, :], "xTh")

                def exps(r):
                    ev.wait(eng, "xr", r)
                    ev.did(eng.activation(t2[:, r % 2, :], t1[:, r % 2, :], ACT.Relu, scale=-1.0), "r")
                    ev.wait(eng, "r", r)
                    ev.did(eng.activation(e[:, r % 2, :], t2[:, r % 2, :], ACT.Exp, scale=-1.0), "e")

                def v_high(c):
                    ev.wait(eng, "pq", unit_v(c))
                    if c >= 2:
                        ev.wait(eng, "out", 4 * (c - 2) + 3)
                        ev.wait(eng, "u", c - 2)
                    copy(V_h[:, c % 2, :], PQ[unit_v(c) % 2][:, :], "Vh")

                def k_high(c):
                    ev.wait(eng, "f", rot_k(c))
                    ev.wait(eng, "u", c - 1)
                    ev.wait(eng, "zc", c - 1)
                    copy(K_h[:, :], fK[:, :], "Kh")

                def z_high(c):
                    ev.wait(eng, "zc", c)
                    copy(z_h[:, :], PM[:, :], "zh")
                    ev.wait(eng, "m", 4 * (c - 1) + 3)
                    copy(z[:, :], PM[:, :], "z")

                def turn_high(j):
                    kind, i = turns[j]
                    h = KT_h if kind == "TK" else QT_h
                    ev.wait(eng, "pt", j)
                    if kind == "TK":
                        ev.wait(eng, "sc", 4 * (i - 2) + 3)
                    else:
                        ev.wait(eng, "out", i - 2)
                    copy(h[:, i % 2, :], PT[j % 2][:, :], "th")

                def a_high(n):
                    ev.wait(eng, "A", n)
                    ev.wait(eng, "out", n - 2)
                    copy(A_h[:, n % 2, :], A[:, n % 2, :], "Ah")

                def s_high(c):
                    ev.wait(eng, "S", c)
                    ev.wait(eng, "out", 4 * (c - 1) + 3)
                    copy(S_h[:, (c + 1) % 2, :], S[:, :], "Sh")

                def out(n):
                    ev.wait(eng, "out", n)
                    if n >= 2:
                        ev.wait(eng, f"oT{n % 2}", n // 2 - 1, 16)
                    copy(o[:, n % 2, :], PO[:, :], "o")

                weight_high(0)
                xT_high(0)
                for i in range(1, 12):
                    weight_high(i)
                for n in range(NG + 5):
                    c, g = divmod(n, 4)
                    if g == 0 and c < NC:
                        exps(rot_k(c))
                        v_high(c)
                    if 0 <= n - 5 < NG:
                        out(n - 5)
                    if g == 0 and c < NC:
                        k_high(c)
                    if n < NG:
                        exps(rot_q(n))
                    if g == 0 and 1 <= c < NC:
                        s_high(c - 1)
                    if c == 0 and g < 3:
                        for i in range(12 + 4 * g, 16 + 4 * g):
                            weight_high(i)
                    if g == 1 and c < NC:
                        turn_high(turn[("TK", c)])
                        z_high(c)
                    if 0 <= n - 3 < NG:
                        turn_high(turn[("T", n - 3)])
                    if g == 2 and c + 1 < NC:
                        xT_high(c + 1)
                    if 0 <= n - 4 < NG:
                        a_high(n - 4)

            @block.gpsimd
            def _(eng):
                def rstd(c):
                    ev.wait(eng, "mv", c)
                    ev.wait(eng, "neg", 0)
                    ev.wait(eng, "xn", c - 2)
                    ev.did(eng.tensor_scalar_add(vr[:, c % 2, 0:1], mv[:, c % 2, 1:2], 1e-5), "ve")
                    ev.wait(eng, "ve", c)
                    ev.did(eng.tensor_tensor(vr[:, c % 2, 1:2], vr[:, c % 2, 0:1], neg[:, :], ALU.pow), "rstd")

                def add(r):
                    c, i = divmod(r, 5)
                    ev.wait(eng, "pqfree", 6 * c + (0 if i == 0 else i + 1))
                    ev.did(eng.tensor_tensor(t1[:, r % 2, :], t1[:, r % 2, :], t2[:, r % 2, :], ALU.add), "xr")

                def k_low(c):
                    ev.wait(eng, "Kh", c)
                    ev.did(eng.tensor_tensor(K_l[:, :], fK[:, :], f(K_h[:, :]), ALU.subtract), "Kl")

                def s_low(c):
                    ev.wait(eng, "Sh", c)
                    ev.did(eng.tensor_tensor(S_l[:, (c + 1) % 2, :], S[:, :], f(S_h[:, (c + 1) % 2, :]),
                                             ALU.subtract), "Sl")

                def times_z(n):
                    ev.wait(eng, "f", rot_q(n))
                    ev.wait(eng, "z", n // 4)
                    ev.wait(eng, "den", n - 1)
                    g = n % 4
                    ev.did(eng.tensor_tensor(heads(m[:, :]), heads(fQ[:, n % 3, :]),
                                             spread(z[:, g * P:(g + 1) * P]), ALU.mult), "m")

                def scale(n):
                    ev.wait(eng, "rden", n)
                    q = heads(fQ[:, n % 3, :])
                    ev.did(eng.tensor_tensor(q, q, den[:, n % 2, :].unsqueeze(2).broadcast_to([P, 4, P]),
                                             ALU.mult), "fs")

                def a_low(n):
                    ev.wait(eng, "Ah", n)
                    ev.wait(eng, "out", n - 2)
                    ev.did(eng.tensor_tensor(A_l[:, n % 2, :], A[:, n % 2, :], f(A_h[:, n % 2, :]),
                                             ALU.subtract), "Al")

                rstd(0)
                for n in range(NG + 5):
                    c, g = divmod(n, 4)
                    if g == 0 and c < NC:
                        add(rot_k(c))
                    if 0 <= n - 2 < NG:
                        times_z(n - 2)
                    if n < NG:
                        add(rot_q(n))
                    if g == 0 and c < NC:
                        k_low(c)
                    if g == 0 and 1 <= c < NC:
                        s_low(c - 1)
                    if g == 0 and c + 1 < NC:
                        rstd(c + 1)
                    if 0 <= n - 2 < NG:
                        scale(n - 2)
                    if 0 <= n - 4 < NG:
                        a_low(n - 4)


def routing(nc, ev, x, wo, wc, bias, consts, oT, xn2d, out, tbd, gi, si, wt):
    with ExitStack() as ctx:
        def sb(name, shape, dt=F32):
            return ctx.enter_context(nc.sbuf_tensor("r_" + name, shape, dt))

        def ps(name):
            return ctx.enter_context(nc.psum_tensor("r_" + name, [P, 512], F32))

        BF = mybir.dt.bfloat16
        wo_h = sb("wo_h", [P, NH, 512], F32R)
        wo_l = sb("wo_l", [P, NH, 512], F32R)
        wc_s = sb("wc_s", [P, 4, E2])
        wc_h = sb("wc_h", [P, 4, E2], F32R)
        wc_l = sb("wc_l", [P, 4, E2], F32R)
        bs = sb("bs", [P, E2])
        cst = sb("cst", [P, CW])
        o = sb("o", [P, 2, NH * P])
        o_h = sb("o_h", [P, NH * P], F32R)
        o_l = sb("o_l", [P, NH * P], F32R)
        stg = sb("stg", [P, 4, 512])
        xr = sb("xr", [P, 2, D])
        x2 = sb("x2", [P, 2, D])
        xn = sb("xn", [P, 2, D])
        xT_h = sb("xT_h", [P, 4, P], F32R)
        xT_l = sb("xT_l", [P, 4, P], F32R)
        st = sb("st", [P, 6])
        mv = sb("mv", [P, 2])
        vr = sb("vr", [P, 2])
        neg = sb("neg", [P, 1])
        c1 = sb("c1", [P, 16])
        ex = sb("ex", [P, E2])
        zz = sb("zz", [P, E2])
        top = sb("top", [P, 8])
        zr = sb("zr", [P, E2])
        mask = sb("mask", [P, E2])
        maskb = sb("maskb", [P, NE], BF)
        macc = sb("macc", [P, NE])
        maccb = sb("maccb", [P, NE], BF)
        trib = sb("trib", [P, P], BF)
        oneb = sb("oneb", [P, P], BF)
        ws = sb("ws", [P, E2])
        w = sb("w", [P, NE])
        w_h = sb("w_h", [P, 2, NE], F32R)
        w_l = sb("w_l", [P, 2, NE])
        rk = sb("rk", [P, NE])
        rki = sb("rki", [P, NE], I32)
        ra = sb("ra", [P, NE], I32)
        rb = sb("rb", [P, NE], I32)
        OA = sb("OA", [P, 2, 512], F32R)
        OB = sb("OB", [P, 512])
        mvv = sb("mvv", [P, 2, 3, 512], F32R)
        tmp = sb("tmp", [P, 2, P])
        R = sb("R", [P, 2, 4, 16])
        tb = sb("tb", [64, 2, P])
        id0 = sb("id0", [P, 64])
        id1 = sb("id1", [P, 64])
        tidc = sb("tidc", [P, NC])

        PY = [ps("PY0"), ps("PY1")]
        PX, PR = ps("PX"), ps("PR")
        PB = [ps(f"PB{g}") for g in range(4)]

        ident = cst[:, 0:128]
        stri = cst[:, 128:256]
        iota = cst[:, 256:272]
        tid = cst[:, 272:273]
        dump = cst[:, 273:274]
        blk = cst[:, 274:282]

        def f(ap):
            return ap.bitcast(F32)

        def flat(ap):
            return ap.rearrange("p k t -> p (k t)")

        def by16(ap):
            return ap.rearrange("p (e b) -> p e b", b=16)

        def wide(ap):
            return ap.unsqueeze(2).broadcast_to([P, NE, 16])

        with nc.Block() as block:
            @block.sync
            def _(eng):
                def load(c):
                    ev.wait(eng, "r_ol", c - 2)
                    ev.did(eng.dma_start(o[:, c % 2, :], oT[c].rearrange("d h t -> d (h t)")), f"r_o{c % 2}", 16)
                    ev.wait(eng, "r_x2", c - 2)
                    ev.did(eng.dma_start(xr[:, c % 2, :], x[c * P:(c + 1) * P, :]), f"r_x{c % 2}", 16)

                ev.did(eng.dma_start(cst[:, :], consts), "r_cst", 16)
                for i in range(4):
                    ev.did(eng.dma_start(stg[:, i, :], wo[i * P:(i + 1) * P, :]), f"r_st{i}", 16)
                load(0)
                ev.did(eng.dma_start(wc_s[:, :, :], wc.rearrange("(k p) e -> p k e", p=P)), "r_wc", 16)
                ev.did(eng.dma_start(bs[:, :], bias.rearrange("(a e) -> a e", a=1).broadcast_to([P, E2])), "r_b", 16)
                for i in range(4, NH):
                    ev.wait(eng, "r_wol", i - 4)
                    ev.did(eng.dma_start(stg[:, i % 4, :], wo[i * P:(i + 1) * P, :]), f"r_st{i % 4}", 16)
                load(1)
                for c in range(NC):
                    rows = slice(c * P, (c + 1) * P)
                    ev.wait(eng, "r_x2", c)
                    ev.did(eng.dma_start(out[rows, :], x2[:, c % 2, :]), f"r_so{c % 2}", 16)
                    ev.wait(eng, "r_xn", c)
                    ev.did(eng.dma_start(xn2d[rows, :], xn[:, c % 2, :]), f"r_sx{c % 2}", 16)
                    if c + 2 < NC:
                        load(c + 2)
                ev.did(eng.dma_start(out[T:T + P, :], x2[:, 1, :]), "r_so1", 16)
                ev.wait(eng, "r_R", 7)
                for v in range(2):
                    ev.did(eng.dma_start(tbd[v].rearrange("(g p b) -> p g b", p=P, b=16), R[:, v, :, :]), "r_tw", 16)
                ev.wait(eng, "r_tw", 1, 16)
                ev.did(eng.dma_start(tb[:, :, :], tbd.rearrange("v (t s) -> t v s", s=P)), "r_tb", 16)
                ev.wait(eng, "r_tb", 0, 16)
                for b in range(2):
                    ev.wait(eng, f"r_so{b}", NC // 2 - 1 + b, 16)
                    ev.wait(eng, f"r_sx{b}", NC // 2 - 1, 16)

            @block.tensor
            def _(eng):
                def project(c):
                    ev.wait(eng, "r_x2", c - 2)
                    ev.wait(eng, "r_ol", c)
                    steps = [(o_h, wo_h), (o_h, wo_l), (o_l, wo_h)]
                    for h in range(NH):
                        if c == 0:
                            ev.wait(eng, "r_wol", h)
                        for s, (a, b) in enumerate(steps):
                            last = eng.matmul(PY[c % 2][:, :], a[:, h * P:(h + 1) * P], b[:, h, :],
                                              start=h == 0 and s == 0, stop=h == NH - 1 and s == 2)
                    ev.did(last, "r_y")

                def turn(c):
                    ev.wait(eng, "r_cst", 0, 16)
                    ev.wait(eng, "r_xTl", c - 1)
                    ev.wait(eng, "r_xn", c)
                    for k in range(4):
                        last = eng.transpose(PX[:, k * P:(k + 1) * P], xn[:, c % 2, k * P:(k + 1) * P], ident)
                    ev.did(last, "r_xt")

                def logits(c):
                    ev.wait(eng, "r_wcl", 0)
                    ev.wait(eng, "r_xTl", c)
                    ev.wait(eng, "r_rk", c - 1)
                    steps = [(xT_h, wc_h), (xT_h, wc_l), (xT_l, wc_h)]
                    for s, (a, b) in enumerate(steps):
                        for k in range(4):
                            last = eng.matmul(PR[:, 0:E2], a[:, k, :], b[:, k, :],
                                              start=s == 0 and k == 0, stop=s == 2 and k == 3)
                    ev.did(last, "r_lg")

                def ranks(c):
                    ev.wait(eng, "r_e", c)
                    ev.wait(eng, "r_mb", c)
                    last = eng.matmul(PR[:, 128:128 + NE], trib[:, :], maskb[:, :], start=True, stop=c == 0)
                    if c > 0:
                        ev.wait(eng, "r_mab", c - 1)
                        last = eng.matmul(PR[:, 128:128 + NE], oneb[:, :], maccb[:, :], start=False, stop=True)
                    ev.did(last, "r_rank")

                def table(c):
                    ev.wait(eng, "r_mv", c)
                    for g in range(4):
                        cols = slice(g * P, (g + 1) * P)
                        a = OA[:, c % 2, cols]
                        eng.matmul(PB[g][:, 0:256], a, mvv[:, c % 2, 0:2, cols], start=c == 0, stop=False)
                        last = eng.matmul(PB[g][:, 128:256], a, mvv[:, c % 2, 2, cols], start=False,
                                          stop=c == NC - 1)
                    ev.did(last, "r_tbl")

                for c in range(NC + 3):
                    if c < NC:
                        project(c)
                    if 0 <= c - 1 < NC:
                        turn(c - 1)
                    if 0 <= c - 2 < NC:
                        ranks(c - 2)
                    if 0 <= c - 1 < NC:
                        logits(c - 1)
                    if c >= 3:
                        table(c - 3)
                ev.wait(eng, "r_tb", 0, 16)
                ev.wait(eng, "r_xTl", NC - 1)
                for v in range(2):
                    last = eng.transpose(PX[:, 64 * v:64 * v + 64], tb[:, v, :], cst[0:64, 0:64])
                ev.did(last, "r_tt")

            @block.vector
            def _(eng):
                chain = [0]

                def then(ins):
                    ev.did(ins, "r_dve")
                    ev.wait(eng, "r_dve", chain[0])
                    chain[0] += 1

                def low(i):
                    ev.wait(eng, "r_woh", i)
                    ev.did(eng.tensor_tensor(wo_l[:, i, :], stg[:, i % 4, :], f(wo_h[:, i, :]), ALU.subtract), "r_wol")

                def o_low(c):
                    ev.wait(eng, "r_oh", c)
                    ev.did(eng.tensor_tensor(o_l[:, :], o[:, c % 2, :], f(o_h[:, :]), ALU.subtract), "r_ol")

                def residual(c):
                    ev.wait(eng, "r_y", c)
                    ev.wait(eng, f"r_x{c % 2}", c // 2, 16)
                    if c >= 2:
                        ev.wait(eng, f"r_so{c % 2}", c // 2 - 1, 16)
                    ev.did(eng.tensor_tensor(x2[:, c % 2, :], PY[c % 2][:, :], xr[:, c % 2, :], ALU.add), "r_x2")
                    ev.wait(eng, "r_x2", c)
                    then(eng.bn_stats(st[:, :], x2[:, c % 2, :]))
                    ev.did(eng.bn_aggr(mv[:, :], st[:, :]), "r_mvd")

                def normal(c):
                    ev.wait(eng, "r_rstd", c)
                    ev.wait(eng, "r_xt", c - 2)
                    if c >= 2:
                        ev.wait(eng, f"r_sx{c % 2}", c // 2 - 1, 16)
                    ev.did(eng.tensor_scalar(xn[:, c % 2, :], x2[:, c % 2, :], mv[:, 0:1], vr[:, 1:2],
                                             ALU.subtract, ALU.mult), "r_xn")

                def xT_low(c):
                    ev.wait(eng, "r_xTh", c)
                    ev.did(eng.tensor_tensor(flat(xT_l[:, :, :]), PX[:, :], f(flat(xT_h[:, :, :])), ALU.subtract), "r_xTl")

                def choose(c):
                    ev.wait(eng, "r_lg", c)
                    then(eng.tensor_reduce(c1[:, 0:1], PR[:, 0:E2], axis=AX, op=ALU.max))
                    ev.did(eng.tensor_scalar(c1[:, 1:2], c1[:, 0:1], -1.0, None, ALU.mult), "r_nm")
                    ev.wait(eng, "r_e", c)
                    then(eng.reciprocal(c1[:, 3:4], c1[:, 2:3]))
                    ev.wait(eng, "r_b", 0, 16)
                    then(eng.scalar_tensor_tensor(out=zz[:, :], in0=ex[:, :], scalar=c1[:, 3:4], in1=bs[:, :],
                                                  op0=ALU.mult, op1=ALU.add))
                    then(eng.max(top[:, :], zz[:, :]))
                    then(eng.match_replace(out=zr[:, :], in_to_replace=top[:, :], in_values=zz[:, :], imm_value=-3e38))
                    eng.tensor_tensor(mask[:, :], zr[:, :], zz[:, :], ALU.not_equal)
                    ev.wait(eng, "r_rank", c - 1)
                    ev.did(eng.tensor_tensor(maskb[:, :], zr[:, 0:NE], zz[:, 0:NE], ALU.not_equal), "r_mb")
                    ev.wait(eng, "r_mb", c)
                    then(eng.scalar_tensor_tensor(out=ws[:, :], in0=ex[:, :], scalar=c1[:, 3:4], in1=mask[:, :],
                                                  op0=ALU.mult, op1=ALU.mult))
                    eng.tensor_reduce(c1[:, 4:5], ws[:, :], axis=AX, op=ALU.add)
                    then(eng.tensor_reduce(c1[:, 5:6], ws[:, NE:E2], axis=AX, op=ALU.add))
                    then(eng.tensor_scalar(c1[:, 6:7], c1[:, 4:5], 1e-20, None, ALU.add))
                    then(eng.reciprocal(c1[:, 7:8], c1[:, 6:7]))
                    then(eng.tensor_scalar(c1[:, 8:9], c1[:, 7:8], 1.5, None, ALU.mult))
                    then(eng.tensor_scalar(c1[:, 9:10], c1[:, 5:6], c1[:, 8:9], 1.0, ALU.mult, ALU.add))
                    then(eng.tensor_scalar(w[:, :], ws[:, 0:NE], c1[:, 8:9], c1[:, 9:10], ALU.mult, ALU.mult))
                    ev.wait(eng, "r_mv", c - 2)
                    then(eng.tensor_copy(w_h[:, c % 2, :], w[:, :]))
                    ev.did(eng.tensor_tensor(w_l[:, c % 2, :], w[:, :], f(w_h[:, c % 2, :]), ALU.subtract), "r_wl")

                def slots(c):
                    ev.wait(eng, "r_rank", c)
                    if c == 0:
                        then(eng.tensor_copy(macc[:, :], mask[:, 0:NE]))
                    else:
                        then(eng.tensor_tensor(macc[:, :], macc[:, :], mask[:, 0:NE], ALU.add))
                    ev.did(eng.tensor_copy(maccb[:, :], macc[:, :]), "r_mab")
                    ev.did(eng.scalar_tensor_tensor(out=rk[:, :], in0=mask[:, 0:NE], scalar=-4096.0,
                                                    in1=PR[:, 128:128 + NE], op0=ALU.mult, op1=ALU.add), "r_rk")
                    ev.wait(eng, "r_rk", c)
                    then(eng.tensor_scalar(rki[:, :], rk[:, :], 4096.0, None, ALU.add))
                    eng.tensor_scalar(ra[:, :], rki[:, :], 4, None, ALU.arith_shift_right)
                    then(eng.tensor_scalar(rb[:, :], rki[:, :], 15, None, ALU.bitwise_and))
                    io = iota.unsqueeze(1).broadcast_to([P, NE, 16])
                    ev.wait(eng, "r_tbl", c - 2)
                    eng.tensor_tensor(by16(OA[:, c % 2, :]), wide(ra[:, :]), io, ALU.is_equal)
                    ev.wait(eng, "r_mv", c - 1)
                    ev.did(eng.tensor_tensor(by16(OB[:, :]), wide(rb[:, :]), io, ALU.is_equal), "r_OB")

                ev.did(eng.memset(neg[:, :], -0.5), "r_neg")
                eng.memset(oneb[:, :], 1.0)
                ev.wait(eng, "r_cst", 0, 16)
                then(eng.tensor_copy(trib[:, :], stri))
                for i in range(4):
                    low(i)
                o_low(0)
                for i in range(4, NH):
                    low(i)
                ev.wait(eng, "r_wch", 0)
                ev.did(eng.tensor_tensor(flat(wc_l[:, :, :]), flat(wc_s[:, :, :]), f(flat(wc_h[:, :, :])), ALU.subtract), "r_wcl")
                for c in range(NC + 1):
                    if c < NC:
                        residual(c)
                        normal(c)
                        if c + 1 < NC:
                            ev.wait(eng, "r_y", c)
                            o_low(c + 1)
                        xT_low(c)
                    if c >= 1:
                        slots(c - 1)
                    if c < NC:
                        choose(c)
                for g in range(4):
                    ev.wait(eng, "r_tbl", NC - 1)
                    b4 = blk.unsqueeze(2).broadcast_to([P, 8, 16])
                    for v in range(2):
                        then(eng.tensor_tensor(tmp[:, v, :].rearrange("p (e b) -> p e b", b=16),
                                               PB[g][:, v * P:(v + 1) * P].rearrange("p (e b) -> p e b", b=16),
                                               b4, ALU.mult))
                        ev.did(eng.tensor_reduce(R[:, v, g, :], tmp[:, v, :].rearrange("p (e b) -> p b e", b=16),
                                                 axis=AX, op=ALU.add), "r_R")
                ev.wait(eng, "r_tt", 0)
                ids, wts = PX[:, 0:64], PX[:, 64:128]
                eng.tensor_copy(wt[:, :], wts)
                then(eng.tensor_scalar(id0[:, :], ids, 0.0, None, ALU.is_equal))
                then(eng.tensor_scalar(id0[:, :], id0[:, :], dump, None, ALU.mult))
                eng.tensor_scalar(gi[:, :], ids, -1.0, 0.0, ALU.add, ALU.max)
                then(eng.tensor_scalar(id1[:, :], ids, -1.0, None, ALU.add))
                then(eng.tensor_tensor(si[:, :], id0[:, :], id1[:, :], ALU.add))

            @block.scalar
            def _(eng):
                def copy(out_, in_, kind):
                    ev.did(eng.activation(out_, in_, ACT.Copy), kind)

                def high(i):
                    ev.wait(eng, f"r_st{i % 4}", i // 4, 16)
                    copy(wo_h[:, i, :], stg[:, i % 4, :], "r_woh")

                def o_high(c):
                    ev.wait(eng, "r_y", c - 1)
                    ev.wait(eng, f"r_o{c % 2}", c // 2, 16)
                    copy(o_h[:, :], o[:, c % 2, :], "r_oh")

                for i in range(4):
                    high(i)
                o_high(0)
                for i in range(4, NH):
                    high(i)
                ev.wait(eng, "r_wc", 0, 16)
                copy(flat(wc_h[:, :, :]), flat(wc_s[:, :, :]), "r_wch")
                for c in range(NC):
                    if c + 1 < NC:
                        o_high(c + 1)
                    ev.wait(eng, "r_xt", c)
                    ev.wait(eng, "r_lg", c - 1)
                    copy(flat(xT_h[:, :, :]), PX[:, :], "r_xTh")
                    ev.wait(eng, "r_nm", c)
                    ev.did(eng.activation(ex[:, :], PR[:, 0:E2], ACT.Exp, bias=c1[:, 1:2], accum_out=c1[:, 2:3]), "r_e")

            @block.gpsimd
            def _(eng):
                def rstd(c):
                    ev.wait(eng, "r_mvd", c)
                    ev.wait(eng, "r_neg", 0)
                    ev.did(eng.tensor_scalar_add(vr[:, 0:1], mv[:, 1:2], 1e-5), "r_ve")
                    ev.wait(eng, "r_ve", c)
                    ev.did(eng.tensor_tensor(vr[:, 1:2], vr[:, 0:1], neg[:, :], ALU.pow), "r_rstd")

                def values(c):
                    ev.wait(eng, "r_OB", c)
                    ev.wait(eng, "r_tbl", c - 2)
                    ob = by16(OB[:, :])
                    ev.did(eng.tensor_scalar(tidc[:, c:c + 1], tid, float(c * P), None, ALU.add), "r_tid")
                    ev.wait(eng, "r_tid", c)
                    eng.tensor_scalar(mvv[:, c % 2, 0, :], OB[:, :], tidc[:, c:c + 1], None, ALU.mult)
                    ev.wait(eng, "r_wl", c)
                    eng.tensor_tensor(by16(mvv[:, c % 2, 1, :]), ob, wide(f(w_h[:, c % 2, :])), ALU.mult)
                    ev.did(eng.tensor_tensor(by16(mvv[:, c % 2, 2, :]), ob, wide(w_l[:, c % 2, :]), ALU.mult), "r_mv")

                for c in range(NC + 1):
                    if c < NC:
                        rstd(c)
                    if c >= 1:
                        values(c - 1)


def experts(nc, ev, wgu, wd, xn2d, out, gi, si, wt, consts):
    with ExitStack() as ctx:
        def sb(name, shape, dt=F32):
            return ctx.enter_context(nc.sbuf_tensor("m_" + name, shape, dt))

        def ps(name):
            return ctx.enter_context(nc.psum_tensor("m_" + name, [P, 512], F32))

        raw = sb("raw", [P, 3, 6, 512])
        w_h = sb("w_h", [P, 3, 6, 512], F32R)
        w_l = sb("w_l", [P, 3, 6, 512], F32R)
        xg = sb("xg", [P, 4, 2, D])
        xT_h = sb("xT_h", [P, 2, 2, 512], F32R)
        xT_l = sb("xT_l", [P, 2, 2, 512], F32R)
        s = sb("s", [P, 2, 512])
        a = sb("a", [P, 2, 512])
        a_h = sb("a_h", [P, 2, 512], F32R)
        a_l = sb("a_l", [P, 2, 512], F32R)
        y = sb("y", [P, 2, 2, D])
        ident = sb("ident", [P, P])
        PX = [ps("PX0"), ps("PX1")]
        PG, PU = [ps("PG0"), ps("PG1")], [ps("PU0"), ps("PU1")]
        PY = [ps("PY0"), ps("PY1")]

        def f(ap):
            return ap.bitcast(F32)

        def flat(ap):
            return ap.rearrange("p k t -> p (k t)")

        with nc.Block() as block:
            @block.sync
            def _(eng):
                ev.did(eng.dma_start(ident[:, :], consts[:, 0:128]), "m_id", 16)
                for e in range(NE):
                    ev.wait(eng, "m_wl", 2 * (e - 3) + 1)
                    ev.did(eng.dma_start(raw[:, e % 3, 0:4, :], wgu[e].rearrange("(k p) f -> p k f", p=P)),
                           f"m_wg{e % 3}", 16)
                    ev.did(eng.dma_start(raw[:, e % 3, 4:6, :], wd[e].rearrange("(k p) f -> p k f", p=P)),
                           f"m_wd{e % 3}", 16)

            @block.gpsimd
            def _(eng):
                def gather(e):
                    ev.wait(eng, "m_xt", e - 4)
                    for t in range(2):
                        i = 2 * e + t
                        ev.did(eng.indirect_dma_start(
                            xg[:, e % 4, t, :], None, xn2d[:, :],
                            bass.IndirectOffsetOnAxis(ap=gi[:, i:i + 1], axis=0)), f"m_g{e % 4}", 16)

                def scatter(e):
                    for t in range(2):
                        i = 2 * e + t
                        ev.wait(eng, "m_y", i)
                        ev.wait(eng, "m_s", i - 1, 16)
                        ev.did(eng.indirect_dma_start(
                            out[:, :], bass.IndirectOffsetOnAxis(ap=si[:, i:i + 1], axis=0),
                            y[:, e % 2, t, :], None, compute_op=ALU.add), "m_s", 16)

                for e in range(4):
                    gather(e)
                for e in range(NE):
                    scatter(e)
                    if e + 4 < NE:
                        gather(e + 4)
                ev.wait(eng, "m_s", 2 * NE - 1, 16)

            @block.tensor
            def _(eng):
                def turn(e):
                    ev.wait(eng, "m_id", 0, 16)
                    ev.wait(eng, f"m_g{e % 4}", 2 * (e // 4) + 1, 16)
                    ev.wait(eng, "m_xTl", 2 * (e - 1) + 1)
                    for t in range(2):
                        for k in range(4):
                            last = eng.transpose(PX[t][:, k * P:(k + 1) * P], xg[:, e % 4, t, k * P:(k + 1) * P],
                                                 ident[:, :])
                    ev.did(last, "m_xt")

                def up(e):
                    ev.wait(eng, "m_xTl", 2 * e + 1)
                    ev.wait(eng, "m_a", e - 2)
                    ev.wait(eng, "m_wl", 2 * e)
                    xh, xl = (b[:, e % 2].rearrange("p t (k s) -> p t k s", k=4) for b in (xT_h, xT_l))
                    steps = [(w_h, xh), (w_l, xh), (w_h, xl)]
                    for fb in range(4):
                        bank = (PG, PU)[fb // 2][e % 2]
                        dst = bank[:, (fb % 2) * 256:(fb % 2) * 256 + 256]
                        for i, (wt_, xt) in enumerate(steps):
                            for k in range(4):
                                last = eng.matmul(dst, wt_[:, e % 3, k, fb * P:(fb + 1) * P], xt[:, :, k, :],
                                                  start=i == 0 and k == 0, stop=i == 2 and k == 3)
                    ev.did(last, "m_gu")

                def down(e):
                    ev.wait(eng, "m_al", e)
                    ev.wait(eng, "m_wl", 2 * e + 1)
                    steps = [(a_h, w_h), (a_h, w_l), (a_l, w_h)]
                    for t in range(2):
                        ev.wait(eng, "m_y", 2 * (e - 1) + t)
                        for i, (at, w) in enumerate(steps):
                            for b in range(2):
                                last = eng.matmul(PY[t][:, :], at[:, e % 2, b * 256 + t * P:b * 256 + (t + 1) * P],
                                                  w[:, e % 3, 4 + b, :], start=i == 0 and b == 0,
                                                  stop=i == 2 and b == 1)
                        ev.did(last, "m_yd")

                turn(0)
                for e in range(NE + 1):
                    if e < NE:
                        up(e)
                    if e + 1 < NE:
                        turn(e + 1)
                    if e >= 1:
                        down(e - 1)

            @block.vector
            def _(eng):
                def w_low(e):
                    for j, (r, kind) in enumerate(((slice(0, 4), "g"), (slice(4, 6), "d"))):
                        ev.wait(eng, "m_wh", 2 * e + j)
                        ev.did(eng.tensor_tensor(flat(w_l[:, e % 3, r, :]), flat(raw[:, e % 3, r, :]),
                                                 f(flat(w_h[:, e % 3, r, :])), ALU.subtract), "m_wl")

                def x_low(e):
                    for t in range(2):
                        ev.wait(eng, "m_xTh", 2 * e + t)
                        ev.did(eng.tensor_tensor(xT_l[:, e % 2, t, :], PX[t][:, :], f(xT_h[:, e % 2, t, :]),
                                                 ALU.subtract), "m_xTl")

                def act(e):
                    ev.wait(eng, "m_si", e)
                    ev.did(eng.tensor_tensor(a[:, e % 2, :], PU[e % 2][:, :], s[:, e % 2, :], ALU.mult), "m_a")
                    ev.wait(eng, "m_ah", e)
                    ev.did(eng.tensor_tensor(a_l[:, e % 2, :], a[:, e % 2, :], f(a_h[:, e % 2, :]), ALU.subtract), "m_al")

                w_low(0)
                x_low(0)
                w_low(1)
                for e in range(NE):
                    if e + 1 < NE:
                        x_low(e + 1)
                    act(e)
                    if e + 2 < NE:
                        w_low(e + 2)

            @block.scalar
            def _(eng):
                def copy(out_, in_, kind):
                    ev.did(eng.activation(out_, in_, ACT.Copy), kind)

                def w_high(e):
                    for j, r in enumerate((slice(0, 4), slice(4, 6))):
                        ev.wait(eng, f"m_w{'gd'[j]}{e % 3}", e // 3, 16)
                        ev.wait(eng, "m_gu", e - 3)
                        ev.wait(eng, "m_yd", 2 * (e - 3) + 1)
                        copy(flat(w_h[:, e % 3, r, :]), flat(raw[:, e % 3, r, :]), "m_wh")

                def x_high(e):
                    for t in range(2):
                        ev.wait(eng, "m_xt", e)
                        ev.wait(eng, "m_gu", e - 2)
                        copy(xT_h[:, e % 2, t, :], PX[t][:, :], "m_xTh")

                def act(e):
                    ev.wait(eng, "m_gu", e)
                    ev.did(eng.activation(s[:, e % 2, :], PG[e % 2][:, :], ACT.Silu), "m_si")
                    ev.wait(eng, "m_a", e)
                    copy(a_h[:, e % 2, :], a[:, e % 2, :], "m_ah")

                def weigh(e):
                    for t in range(2):
                        ev.wait(eng, "m_yd", 2 * e + t)
                        ev.wait(eng, "m_s", 2 * (e - 2) + 1, 16)
                        ev.did(eng.activation(y[:, e % 2, t, :], PY[t][:, :], ACT.Copy,
                                              scale=wt[:, 2 * e + t:2 * e + t + 1]), "m_y")

                w_high(0)
                x_high(0)
                w_high(1)
                for e in range(NE + 1):
                    if e + 1 < NE:
                        x_high(e + 1)
                    if e < NE:
                        act(e)
                    if e >= 1:
                        weigh(e - 1)
                    if e + 2 < NE:
                        w_high(e + 2)


def build(nc, x, wq, wk, wv, wo, wc, bias, wgu, wd, tabs, ca, cr, out):
    with ExitStack() as ctx:
        ev = Events(nc, ctx)
        oT = nc.dram_tensor("oT", [NC, P, NH, P], F32).ap()
        xn2d = nc.dram_tensor("xn2d", [T, D], F32).ap()
        tbd = nc.dram_tensor("tbd", [2, 64 * P], F32).ap()
        attention(nc, ev, x, wq, wk, wv, tabs, ca, oT)
        gi = ctx.enter_context(nc.sbuf_tensor("gi", [P, 64], U32))
        si = ctx.enter_context(nc.sbuf_tensor("si", [P, 64], U32))
        wt = ctx.enter_context(nc.sbuf_tensor("wt", [P, 64], F32))
        routing(nc, ev, x, wo, wc, bias, cr, oT, xn2d, out, tbd, gi, si, wt)
        experts(nc, ev, wgu, wd, xn2d, out, gi, si, wt, cr)
        ev.check()


def kernel(L0_attn_x, L0_attn_Wq, L0_attn_Wk, L0_attn_Wv, L0_attn_Wo, L0_ffn_w_cls, L0_ffn_bias,
           L0_ffn_w_gate_up, L0_ffn_w_down):
    import numpy as np
    import concourse.bacc as bacc
    from concourse.bass_utils import run_bass_kernel_spmd

    i = np.arange(P)
    ca = np.stack([np.eye(P), i[:, None] <= i[None, :], np.repeat((i == P - 1)[:, None], P, 1)], 1)
    cr = np.zeros((P, CW))
    cr[:, 0:128] = np.eye(P)
    cr[:, 128:256] = i[:, None] < i[None, :]
    cr[:, 256:272] = np.arange(16)[None]
    cr[:, 272] = i + 1
    cr[:, 273] = T + 1 + i
    cr[:, 274:282] = (i[:, None] // 16) == np.arange(8)[None]
    dim = 128
    freq = np.float32(1.0) / np.power(np.float32(10000.0), np.arange(0, dim, 2, dtype=np.float32) / np.float32(dim))
    ang = np.outer(np.arange(T, dtype=np.float32), freq.astype(np.float32))
    co, sn = np.cos(ang), np.sin(ang)
    tabs = np.stack([np.concatenate([co, co], -1), np.concatenate([-sn, sn], -1)], 1).reshape(NC, P, 2, dim)
    arrays = {
        "x": np.asarray(L0_attn_x).reshape(T, D),
        "wq": np.asarray(L0_attn_Wq).T,
        "wk": np.asarray(L0_attn_Wk).T,
        "wv": np.asarray(L0_attn_Wv).T,
        "wo": np.asarray(L0_attn_Wo).T,
        "wc": np.asarray(L0_ffn_w_cls).T,
        "bias": np.asarray(L0_ffn_bias),
        "wgu": np.asarray(L0_ffn_w_gate_up),
        "wd": np.asarray(L0_ffn_w_down),
        "tabs": tabs.astype(np.float32),
        "ca": ca.astype(np.float32),
        "cr": cr.astype(np.float32),
    }
    arrays = {n: np.ascontiguousarray(a) for n, a in arrays.items()}
    nc = bacc.Bacc("TRN2", target_bir_lowering=False, num_devices=1)
    args = [nc.dram_tensor("in_" + n, a.shape, F32, kind="ExternalInput").ap() for n, a in arrays.items()]
    out = nc.dram_tensor("out", [T + P, D], F32, kind="ExternalOutput").ap()
    build(nc, *args, out)
    r = run_bass_kernel_spmd(nc, [{"in_" + n: a for n, a in arrays.items()}], core_ids=[0])
    return r.results[0]["out"][:T].reshape(1, T, D)
```

```python
from contextlib import ExitStack

import concourse.bass as bass
from concourse import mybir

P = 128
D = 512
T = 2048
NC = T // P
NH = 16
KV = 4
NG = NC * KV
NE = 32
E2 = 64
CW = 282

F32 = mybir.dt.float32
F32R = mybir.dt.float32r
I32 = mybir.dt.int32
U32 = mybir.dt.uint32
ALU = mybir.AluOpType
ACT = mybir.ActivationFunctionType
AX = mybir.AxisListType.X


class Events:

    def __init__(self, nc, ctx):
        self.nc, self.ctx, self.sems, self.seen = nc, ctx, {}, {}
        self.done, self.most = {}, {}

    def sem(self, kind):
        if kind not in self.sems:
            self.sems[kind] = self.ctx.enter_context(self.nc.semaphore("e_" + kind))
        return self.sems[kind]

    def did(self, ins, kind, by=1):
        ins.then_inc(self.sem(kind), by)
        self.done[kind] = self.done.get(kind, 0) + 1

    def wait(self, eng, kind, n, by=1):
        if n < 0:
            return
        key = (id(eng), kind)
        if self.seen.get(key, -1) < n:
            self.seen[key] = n
            self.most[kind] = max(self.most.get(kind, 0), n)
            eng.wait_ge(self.sem(kind), (n + 1) * by)

    def check(self):
        short = {k: (n, self.done.get(k, 0)) for k, n in self.most.items() if n >= self.done.get(k, 0)}
        assert not short, short


def attention(nc, ev, x, wq, wk, wv, tabs, consts, oT):
    with ExitStack() as ctx:
        def sb(name, shape, dt=F32):
            return ctx.enter_context(nc.sbuf_tensor("a_" + name, shape, dt))

        def ps(name):
            return ctx.enter_context(nc.psum_tensor("a_" + name, [P, 512], F32))

        w_h = sb("w_h", [P, 24, 512], F32R)
        w_l = sb("w_l", [P, 24, 512], F32R)
        xin = sb("xin", [P, 2, D])
        xn = sb("xn", [P, D])
        xT_h = sb("xT_h", [P, 2, 4, P], F32R)
        xT_l = sb("xT_l", [P, 2, 4, P], F32R)
        tab = sb("tab", [P, 2, 2, P])
        t1 = sb("t1", [P, 2, 512])
        t2 = sb("t2", [P, 2, 512])
        e = sb("e", [P, 2, 512])
        fK = sb("fK", [P, 512])
        fQ = sb("fQ", [P, 3, 512])
        m = sb("m", [P, 512])
        K_h = sb("K_h", [P, 512], F32R)
        K_l = sb("K_l", [P, 512], F32R)
        V_h = sb("V_h", [P, 3, 512], F32R)
        V_l = sb("V_l", [P, 3, 512], F32R)
        KT_h = sb("KT_h", [P, 2, 512], F32R)
        KT_l = sb("KT_l", [P, 2, 512], F32R)
        QT_h = sb("QT_h", [P, 2, 512], F32R)
        QT_l = sb("QT_l", [P, 2, 512], F32R)
        z = sb("z", [P, 512])
        z_h = sb("z_h", [P, 512], F32R)
        z_l = sb("z_l", [P, 512], F32R)
        A = sb("A", [P, 2, 512])
        A_h = sb("A_h", [P, 2, 512], F32R)
        A_l = sb("A_l", [P, 2, 512], F32R)
        o = sb("o", [P, 2, 512])
        S = sb("S", [P, 512])
        S_h = sb("S_h", [P, 2, 512], F32R)
        S_l = sb("S_l", [P, 2, 512], F32R)
        cst = sb("cst", [P, 3, P])
        tri_r = sb("tri_r", [P, P], F32R)
        last_r = sb("last_r", [P, P], F32R)
        st = sb("st", [P, 2, 6])
        mv = sb("mv", [P, 2, 2])
        vr = sb("vr", [P, 2, 2])
        neg = sb("neg", [P, 1])
        den = sb("den", [P, 2, 4])

        PQ = [ps("PQ0"), ps("PQ1")]
        PT = [ps("PT0"), ps("PT1")]
        PX, PS, PO, PM = ps("PX"), ps("PS"), ps("PO"), ps("PM")

        ident = cst[:, 0, :]
        tri = cst[:, 1, :]

        def f(ap):
            return ap.bitcast(F32)

        def heads(ap):
            return ap.rearrange("p (h d) -> p h d", h=4)

        def spread(ap):
            return ap.unsqueeze(1).broadcast_to([P, 4, ap.shape[-1]])

        def unit_k(c):
            return 6 * c

        def unit_v(c):
            return 6 * c + 1

        def unit_q(n):
            return 6 * (n // 4) + 2 + n % 4

        def rot_k(c):
            return 5 * c

        def rot_q(n):
            return 5 * (n // 4) + 1 + n % 4

        def plan():
            ops = []
            for n in range(NG + 5):
                c, g = divmod(n, 4)
                if g == 0 and c < NC:
                    ops += [("PK", c), ("PV", c)]
                if n < NG:
                    ops.append(("P", n))
                if 0 <= n - 5 < NG:
                    ops.append(("O", n - 5))
                if g == 0 and 1 <= c < NC:
                    ops.append(("U", c - 1))
                if g == 1 and c < NC:
                    ops += [("TK", c), ("ZC", c)]
                if 0 <= n - 3 < NG:
                    ops.append(("T", n - 3))
                if g == 2 and c + 1 < NC:
                    ops.append(("XT", c + 1))
                if 0 <= n - 4 < NG:
                    ops.append(("S", n - 4))
            return ops

        order = plan()
        turns = [op for op in order if op[0] in ("TK", "T")]
        turn = {op: j for j, op in enumerate(turns)}

        def piece(i):
            j, k = divmod(i, 4)
            rows = slice(k * P, (k + 1) * P)
            if j == 0:
                return wk[rows, :]
            if j == 1:
                return wv[rows, :]
            return wq[rows, (j - 2) * 512:(j - 1) * 512]

        def stage(i):
            return (A, o)[i % 4 // 2][:, i % 2, :]

        with nc.Block() as block:
            @block.sync
            def _(eng):
                def load_x(c):
                    ev.wait(eng, "xn", c - 2)
                    ev.did(eng.dma_start(xin[:, c % 2, :], x[c * P:(c + 1) * P, :]), f"x{c % 2}", 16)

                def load_tab(c):
                    if c >= 2:
                        ev.wait(eng, "pqfree", unit_q(4 * (c - 2) + 3))
                    ev.did(eng.dma_start(tab[:, c % 2, :, :], tabs[c]), f"tab{c % 2}", 16)

                load_x(0)
                ev.did(eng.dma_start(cst[:, :, :], consts), "cst", 16)
                for i in range(4):
                    ev.did(eng.dma_start(stage(i), piece(i)), f"st{i % 4}", 16)
                load_tab(0)
                load_x(1)
                load_tab(1)
                for i in range(4, 24):
                    ev.wait(eng, "wl", i - 4)
                    ev.did(eng.dma_start(stage(i), piece(i)), f"st{i % 4}", 16)
                for n in range(NG + 5):
                    c, g = divmod(n, 4)
                    if g == 0 and 1 <= c < NC - 1:
                        load_tab(c + 1)
                    if g == 2 and c + 2 < NC:
                        load_x(c + 2)
                    if n >= 5:
                        i = n - 5
                        ev.wait(eng, "o", i)
                        ev.did(eng.dma_start(oT[i // 4, :, 4 * (i % 4):4 * (i % 4) + 4, :],
                                             heads(o[:, i % 2, :])), f"oT{i % 2}", 16)
                for b in range(2):
                    ev.wait(eng, f"oT{b}", NG // 2 - 1, 16)

            @block.tensor
            def _(eng):
                def project(u, c, i):
                    ev.wait(eng, "pqfree", u - 2)
                    ev.wait(eng, "xTl", c)
                    ev.wait(eng, "wl", 4 * i + 3)
                    bank = PQ[u % 2]
                    xh, xl = xT_h[:, c % 2], xT_l[:, c % 2]
                    last = None
                    steps = [(xh, w_h), (xh, w_l), (xl, w_h)]
                    for s, (a, w) in enumerate(steps):
                        for k in range(4):
                            last = eng.matmul(bank[:, :], a[:, k, :], w[:, 4 * i + k, :],
                                              start=s == 0 and k == 0, stop=s == 2 and k == 3)
                    ev.did(last, "pq")

                def op_PK(c):
                    project(unit_k(c), c, 0)

                def op_PV(c):
                    project(unit_v(c), c, 1)

                def op_P(n):
                    project(unit_q(n), n // 4, 2 + n % 4)

                def op_XT(c):
                    ev.wait(eng, "cst", 0, 16)
                    ev.wait(eng, "xn", c)
                    ev.wait(eng, "xTl", c - 1)
                    for k in range(4):
                        last = eng.transpose(PX[:, k * P:(k + 1) * P], xn[:, k * P:(k + 1) * P], ident)
                    ev.did(last, "xt")

                def turned(src, j):
                    ev.wait(eng, "ptfree", j - 2)
                    for k in range(4):
                        last = eng.transpose(PT[j % 2][:, k * P:(k + 1) * P], src[:, k * P:(k + 1) * P], ident)
                    ev.did(last, "pt")

                def op_TK(c):
                    ev.wait(eng, "f", rot_k(c))
                    turned(fK[:, :], turn[("TK", c)])

                def op_T(n):
                    ev.wait(eng, "fs", n)
                    turned(fQ[:, n % 3, :], turn[("T", n)])

                def op_ZC(c):
                    ev.wait(eng, "trr", 0)
                    ev.wait(eng, "Kl", c)
                    ev.wait(eng, "S", c - 1)
                    eng.matmul(PM[:, :], tri_r[:, :], K_h[:, :], start=True, stop=False)
                    last = eng.matmul(PM[:, :], tri_r[:, :], K_l[:, :], start=False, stop=c == 0)
                    if c > 0:
                        ev.wait(eng, "zl", c - 1)
                        eng.matmul(PM[:, :], last_r[:, :], z_h[:, :], start=False, stop=False)
                        last = eng.matmul(PM[:, :], last_r[:, :], z_l[:, :], start=False, stop=True)
                    ev.did(last, "zc")

                def op_S(n):
                    c, g = divmod(n, 4)
                    ev.wait(eng, "ptfree", max(turn[("T", n)], turn[("TK", c)]))
                    ev.wait(eng, "A", n - 1)
                    kh, kl = (a[:, c % 2, g * P:(g + 1) * P] for a in (KT_h, KT_l))
                    qh, ql = QT_h[:, n % 2, :], QT_l[:, n % 2, :]
                    eng.matmul(PS[:, :], kh, qh, start=True, stop=False)
                    eng.matmul(PS[:, :], kh, ql, start=False, stop=False)
                    ev.did(eng.matmul(PS[:, :], kl, qh, start=False, stop=True), "sc")

                def op_O(n):
                    c, g = divmod(n, 4)
                    ev.wait(eng, "o", n - 1)
                    cols = slice(g * P, (g + 1) * P)
                    if c > 0:
                        ev.wait(eng, "Sl", c - 1)
                        sh, sl = S_h[:, c % 2, cols], S_l[:, c % 2, cols]
                        qh, ql = QT_h[:, n % 2, :], QT_l[:, n % 2, :]
                        eng.matmul(PO[:, :], sh, qh, start=True, stop=False)
                        eng.matmul(PO[:, :], sh, ql, start=False, stop=False)
                        eng.matmul(PO[:, :], sl, qh, start=False, stop=False)
                    ev.wait(eng, "pqfree", unit_v(c))
                    ev.wait(eng, "Al", n)
                    vh, vl = V_h[:, c % 3, cols], V_l[:, c % 3, cols]
                    ah, al = A_h[:, n % 2, :], A_l[:, n % 2, :]
                    eng.matmul(PO[:, :], vh, ah, start=c == 0, stop=False)
                    eng.matmul(PO[:, :], vh, al, start=False, stop=False)
                    ev.did(eng.matmul(PO[:, :], vl, ah, start=False, stop=True), "out")

                def op_U(c):
                    ev.wait(eng, "zl", c)
                    ev.wait(eng, "z", c)
                    ev.wait(eng, "pqfree", unit_v(c))
                    for g in range(4):
                        cols = slice(g * P, (g + 1) * P)
                        steps = [(K_h, V_h), (K_h, V_l), (K_l, V_h)]
                        for s, (a, b) in enumerate(steps):
                            last = eng.matmul(PM[:, cols], a[:, cols], b[:, c % 3, cols],
                                              start=s == 0, stop=s == 2)
                    ev.did(last, "u")

                ops = {"PK": op_PK, "PV": op_PV, "P": op_P, "XT": op_XT, "TK": op_TK, "T": op_T,
                       "ZC": op_ZC, "S": op_S, "O": op_O, "U": op_U}
                op_XT(0)
                for kind, i in order:
                    ops[kind](i)

            @block.vector
            def _(eng):
                ev.did(eng.memset(neg[:, :], -0.5), "neg")
                ev.wait(eng, "cst", 0, 16)
                eng.tensor_copy(tri_r[:, :], tri)
                ev.did(eng.tensor_copy(last_r[:, :], cst[:, 2, :]), "trr")

                def stats(c):
                    ev.wait(eng, f"x{c % 2}", c // 2, 16)
                    ev.did(eng.bn_stats(st[:, c % 2, :], xin[:, c % 2, :]), "bn")
                    ev.wait(eng, "bn", c)
                    ev.wait(eng, "xn", c - 2)
                    ev.did(eng.bn_aggr(mv[:, c % 2, :], st[:, c % 2, :]), "mv")

                def normal(c):
                    ev.wait(eng, "rstd", c)
                    ev.wait(eng, "mv", c)
                    ev.wait(eng, "xt", c - 1)
                    ev.did(eng.tensor_scalar(xn[:, :], xin[:, c % 2, :], mv[:, c % 2, 0:1], vr[:, c % 2, 1:2],
                                             ALU.subtract, ALU.mult), "xn")

                def xT_low(c):
                    ev.wait(eng, "xTh", c)
                    ev.did(eng.tensor_tensor(xT_l[:, c % 2, :, :].rearrange("p k t -> p (k t)"), PX[:, :],
                                             f(xT_h[:, c % 2, :, :]).rearrange("p k t -> p (k t)"),
                                             ALU.subtract), "xTl")

                def weight_low(i):
                    ev.wait(eng, "wh", i)
                    ev.did(eng.tensor_tensor(w_l[:, i, :], stage(i), f(w_h[:, i, :]), ALU.subtract), "wl")

                def rotate(u, r, c):
                    ev.wait(eng, "pq", u)
                    ev.wait(eng, f"tab{c % 2}", c // 2, 16)
                    ev.wait(eng, "f", r - 2)
                    q = heads(PQ[u % 2][:, :])
                    a, b = heads(t1[:, r % 2, :]), heads(t2[:, r % 2, :])
                    sn = tab[:, c % 2, 1, :]
                    eng.tensor_tensor(a, q, spread(tab[:, c % 2, 0, :]), ALU.mult)
                    eng.tensor_tensor(b[:, :, 0:64], q[:, :, 64:128], spread(sn[:, 0:64]), ALU.mult)
                    ev.did(eng.tensor_tensor(b[:, :, 64:128], q[:, :, 0:64], spread(sn[:, 64:128]), ALU.mult), "pqfree")

                def feature(r, out):
                    ev.wait(eng, "e", r)
                    ev.did(eng.scalar_tensor_tensor(out=out, in0=t1[:, r % 2, :], scalar=1.0, in1=e[:, r % 2, :],
                                                    op0=ALU.add, op1=ALU.max), "f")

                def feature_k(c):
                    ev.wait(eng, "Kl", c - 1)
                    ev.wait(eng, "Kh", c - 1)
                    if c >= 1:
                        ev.wait(eng, "pt", turn[("TK", c - 1)])
                    feature(rot_k(c), fK[:, :])

                def feature_q(n):
                    if n >= 3:
                        ev.wait(eng, "pt", turn[("T", n - 3)])
                    feature(rot_q(n), fQ[:, n % 3, :])

                def v_low(c):
                    ev.wait(eng, "out", 4 * (c - 3) + 3)
                    ev.wait(eng, "u", c - 3)
                    ev.wait(eng, "Vh", c)
                    ev.did(eng.tensor_tensor(V_l[:, c % 3, :], PQ[unit_v(c) % 2][:, :], f(V_h[:, c % 3, :]),
                                             ALU.subtract), "pqfree")

                def z_low(c):
                    ev.wait(eng, "z", c)
                    ev.did(eng.tensor_tensor(z_l[:, :], PM[:, :], f(z_h[:, :]), ALU.subtract), "zl")

                def reduce(n):
                    ev.wait(eng, "m", n)
                    ev.wait(eng, "fs", n - 2)
                    d = den[:, n % 2, :]
                    ev.did(eng.tensor_reduce(d, heads(m[:, :]), axis=AX, op=ALU.add), "den")
                    ev.wait(eng, "den", n)
                    ev.did(eng.tensor_scalar_add(d, d, 1e-6), "den1")
                    ev.wait(eng, "den1", n)
                    ev.did(eng.reciprocal(d, d), "rden")

                def turn_low(j):
                    kind, i = turns[j]
                    h, l = (KT_h, KT_l) if kind == "TK" else (QT_h, QT_l)
                    if kind == "TK":
                        ev.wait(eng, "sc", 4 * (i - 2) + 3)
                    else:
                        ev.wait(eng, "out", i - 2)
                    ev.wait(eng, "th", j)
                    ev.did(eng.tensor_tensor(l[:, i % 2, :], PT[j % 2][:, :], f(h[:, i % 2, :]), ALU.subtract),
                           "ptfree")

                def masked(n):
                    ev.wait(eng, "sc", n)
                    ev.wait(eng, "Al", n - 2)
                    ev.wait(eng, "Ah", n - 2)
                    ev.did(eng.tensor_tensor(heads(A[:, n % 2, :]), heads(PS[:, :]), spread(tri), ALU.mult), "A")

                def state(c):
                    ev.wait(eng, "u", c)
                    if c == 0:
                        ins = eng.tensor_copy(S[:, :], PM[:, :])
                    else:
                        ev.wait(eng, "Sh", c - 1)
                        ev.wait(eng, "Sl", c - 1)
                        ins = eng.tensor_tensor(S[:, :], PM[:, :], S[:, :], ALU.add)
                    ev.did(ins, "S")

                stats(0)
                normal(0)
                weight_low(0)
                xT_low(0)
                for i in range(1, 12):
                    weight_low(i)
                rotate(unit_k(0), rot_k(0), 0)
                v_low(0)
                for i in range(12, 24):
                    weight_low(i)
                for n in range(NG + 5):
                    c, g = divmod(n, 4)
                    if g == 0 and 0 < c < NC:
                        rotate(unit_k(c), rot_k(c), c)
                        feature_q(n - 1)
                        v_low(c)
                    if n < NG:
                        rotate(unit_q(n), rot_q(n), c)
                    if g == 0 and c < NC:
                        feature_k(c)
                    if g != 0 and n - 1 < NG or n == NG:
                        feature_q(n - 1)
                    if 0 <= n - 2 < NG:
                        reduce(n - 2)
                    if g == 1 and c < NC:
                        turn_low(turn[("TK", c)])
                    if 0 <= n - 3 < NG:
                        turn_low(turn[("T", n - 3)])
                    if 0 <= n - 4 < NG:
                        masked(n - 4)
                    if g == 1 and c < NC:
                        z_low(c)
                    if g == 0 and 1 <= c < NC:
                        state(c - 1)
                    if g == 0 and c + 1 < NC:
                        stats(c + 1)
                    if g == 1 and c + 1 < NC:
                        normal(c + 1)
                    if g == 2 and c + 1 < NC:
                        xT_low(c + 1)

            @block.scalar
            def _(eng):
                def copy(out, in_, kind):
                    ev.did(eng.activation(out, in_, ACT.Copy), kind)

                def weight_high(i):
                    ev.wait(eng, f"st{i % 4}", i // 4, 16)
                    copy(w_h[:, i, :], stage(i), "wh")

                def xT_high(c):
                    ev.wait(eng, "xt", c)
                    if c >= 2:
                        ev.wait(eng, "pq", unit_q(4 * (c - 2) + 3))
                    copy(xT_h[:, c % 2, :, :].rearrange("p k t -> p (k t)"), PX[:, :], "xTh")

                def exps(r):
                    ev.wait(eng, "xr", r)
                    ev.did(eng.activation(t2[:, r % 2, :], t1[:, r % 2, :], ACT.Relu, scale=-1.0), "r")
                    ev.wait(eng, "r", r)
                    ev.did(eng.activation(e[:, r % 2, :], t2[:, r % 2, :], ACT.Exp, scale=-1.0), "e")

                def v_high(c):
                    ev.wait(eng, "pq", unit_v(c))
                    ev.wait(eng, "out", 4 * (c - 3) + 3)
                    ev.wait(eng, "u", c - 3)
                    copy(V_h[:, c % 3, :], PQ[unit_v(c) % 2][:, :], "Vh")

                def k_high(c):
                    ev.wait(eng, "f", rot_k(c))
                    ev.wait(eng, "u", c - 1)
                    ev.wait(eng, "zc", c - 1)
                    copy(K_h[:, :], fK[:, :], "Kh")

                def z_high(c):
                    ev.wait(eng, "zc", c)
                    copy(z_h[:, :], PM[:, :], "zh")
                    ev.wait(eng, "m", 4 * (c - 1) + 3)
                    copy(z[:, :], PM[:, :], "z")

                def turn_high(j):
                    kind, i = turns[j]
                    h = KT_h if kind == "TK" else QT_h
                    ev.wait(eng, "pt", j)
                    if kind == "TK":
                        ev.wait(eng, "sc", 4 * (i - 2) + 3)
                    else:
                        ev.wait(eng, "out", i - 2)
                    copy(h[:, i % 2, :], PT[j % 2][:, :], "th")

                def a_high(n):
                    ev.wait(eng, "A", n)
                    ev.wait(eng, "out", n - 2)
                    copy(A_h[:, n % 2, :], A[:, n % 2, :], "Ah")

                def s_high(c):
                    ev.wait(eng, "S", c)
                    ev.wait(eng, "out", 4 * (c - 1) + 3)
                    copy(S_h[:, (c + 1) % 2, :], S[:, :], "Sh")

                def out(n):
                    ev.wait(eng, "out", n)
                    if n >= 2:
                        ev.wait(eng, f"oT{n % 2}", n // 2 - 1, 16)
                    copy(o[:, n % 2, :], PO[:, :], "o")

                weight_high(0)
                xT_high(0)
                for i in range(1, 16):
                    weight_high(i)
                v_high(0)
                for i in range(16, 24):
                    weight_high(i)
                for n in range(NG + 5):
                    c, g = divmod(n, 4)
                    if 0 <= n - 1 < NG:
                        exps(rot_q(n - 1))
                    if g == 0 and c < NC:
                        if c > 0:
                            v_high(c)
                        exps(rot_k(c))
                    if 0 <= n - 5 < NG:
                        out(n - 5)
                    if g == 0 and c < NC:
                        k_high(c)
                    if g == 1 and c < NC:
                        turn_high(turn[("TK", c)])
                    if 0 <= n - 3 < NG:
                        turn_high(turn[("T", n - 3)])
                    if g == 1 and c < NC:
                        z_high(c)
                    if g == 2 and c + 1 < NC:
                        xT_high(c + 1)
                    if 0 <= n - 4 < NG:
                        a_high(n - 4)
                    if g == 0 and 1 <= c < NC:
                        s_high(c - 1)

            @block.gpsimd
            def _(eng):
                def rstd(c):
                    ev.wait(eng, "mv", c)
                    ev.wait(eng, "neg", 0)
                    ev.wait(eng, "xn", c - 2)
                    ev.did(eng.tensor_scalar_add(vr[:, c % 2, 0:1], mv[:, c % 2, 1:2], 1e-5), "ve")
                    ev.wait(eng, "ve", c)
                    ev.did(eng.tensor_tensor(vr[:, c % 2, 1:2], vr[:, c % 2, 0:1], neg[:, :], ALU.pow), "rstd")

                def add(r):
                    c, i = divmod(r, 5)
                    ev.wait(eng, "pqfree", 6 * c + (0 if i == 0 else i + 1))
                    ev.did(eng.tensor_tensor(t1[:, r % 2, :], t1[:, r % 2, :], t2[:, r % 2, :], ALU.add), "xr")

                def k_low(c):
                    ev.wait(eng, "Kh", c)
                    ev.did(eng.tensor_tensor(K_l[:, :], fK[:, :], f(K_h[:, :]), ALU.subtract), "Kl")

                def s_low(c):
                    ev.wait(eng, "Sh", c)
                    ev.did(eng.tensor_tensor(S_l[:, (c + 1) % 2, :], S[:, :], f(S_h[:, (c + 1) % 2, :]),
                                             ALU.subtract), "Sl")

                def times_z(n):
                    ev.wait(eng, "f", rot_q(n))
                    ev.wait(eng, "z", n // 4)
                    ev.wait(eng, "den", n - 1)
                    g = n % 4
                    ev.did(eng.tensor_tensor(heads(m[:, :]), heads(fQ[:, n % 3, :]),
                                             spread(z[:, g * P:(g + 1) * P]), ALU.mult), "m")

                def scale(n):
                    ev.wait(eng, "rden", n)
                    q = heads(fQ[:, n % 3, :])
                    ev.did(eng.tensor_tensor(q, q, den[:, n % 2, :].unsqueeze(2).broadcast_to([P, 4, P]),
                                             ALU.mult), "fs")

                def a_low(n):
                    ev.wait(eng, "Ah", n)
                    ev.wait(eng, "out", n - 2)
                    ev.did(eng.tensor_tensor(A_l[:, n % 2, :], A[:, n % 2, :], f(A_h[:, n % 2, :]),
                                             ALU.subtract), "Al")

                rstd(0)
                for n in range(NG + 5):
                    c, g = divmod(n, 4)
                    if 0 <= n - 2 < NG:
                        times_z(n - 2)
                    if g == 0 and c < NC:
                        add(rot_k(c))
                    if n < NG:
                        add(rot_q(n))
                    if g == 0 and c < NC:
                        k_low(c)
                    if 0 <= n - 2 < NG:
                        scale(n - 2)
                    if 0 <= n - 4 < NG:
                        a_low(n - 4)
                    if g == 0 and 1 <= c < NC:
                        s_low(c - 1)
                    if g == 0 and c + 1 < NC:
                        rstd(c + 1)


def routing(nc, ev, x, wo, wc, bias, consts, oT, xn2d, out, tbd, gi, si, wt, raw, wgu, wd):
    with ExitStack() as ctx:
        def sb(name, shape, dt=F32):
            return ctx.enter_context(nc.sbuf_tensor("r_" + name, shape, dt))

        def ps(name):
            return ctx.enter_context(nc.psum_tensor("r_" + name, [P, 512], F32))

        BF = mybir.dt.bfloat16
        wo_h = sb("wo_h", [P, NH, 512], F32R)
        wo_l = sb("wo_l", [P, NH, 512], F32R)
        wc_s = sb("wc_s", [P, 4, E2])
        wc_h = sb("wc_h", [P, 4, E2], F32R)
        wc_l = sb("wc_l", [P, 4, E2], F32R)
        bs = sb("bs", [P, E2])
        cst = sb("cst", [P, CW])
        o = sb("o", [P, 3, NH * P])
        o_h = sb("o_h", [P, 2, NH * P], F32R)
        o_l = sb("o_l", [P, 2, NH * P], F32R)
        stg = sb("stg", [P, 4, 512])
        xr = sb("xr", [P, 2, D])
        x2 = sb("x2", [P, 2, D])
        xn = sb("xn", [P, 2, D])
        xT_h = sb("xT_h", [P, 4, P], F32R)
        xT_l = sb("xT_l", [P, 4, P], F32R)
        st = sb("st", [P, 6])
        mv = sb("mv", [P, 2])
        vr = sb("vr", [P, 2])
        neg = sb("neg", [P, 1])
        c1 = sb("c1", [P, 16])
        ex = sb("ex", [P, E2])
        zz = sb("zz", [P, E2])
        top = sb("top", [P, 8])
        zr = sb("zr", [P, E2])
        mask = sb("mask", [P, E2])
        maskb = sb("maskb", [P, NE], BF)
        macc = sb("macc", [P, NE])
        maccb = sb("maccb", [P, NE], BF)
        trib = sb("trib", [P, P], BF)
        oneb = sb("oneb", [P, P], BF)
        ws = sb("ws", [P, E2])
        w = sb("w", [P, NE])
        w_h = sb("w_h", [P, 2, NE], F32R)
        w_l = sb("w_l", [P, 2, NE])
        rk = sb("rk", [P, NE])
        rki = sb("rki", [P, NE], I32)
        ra = sb("ra", [P, NE], I32)
        rb = sb("rb", [P, NE], I32)
        OA = sb("OA", [P, 2, 512], F32R)
        OB = sb("OB", [P, 512])
        mvv = sb("mvv", [P, 2, 3, 512], F32R)
        tmp = sb("tmp", [P, 2, 8, 16])
        R = sb("R", [P, 2, 4, 16])
        tb = sb("tb", [64, 2, P])
        id0 = sb("id0", [P, 64])
        id1 = sb("id1", [P, 64])
        tidc = sb("tidc", [P, NC])

        PY = [ps("PY0"), ps("PY1")]
        PX, PR = ps("PX"), ps("PR")
        PB = [ps(f"PB{g}") for g in range(4)]

        ident = cst[:, 0:128]
        stri = cst[:, 128:256]
        iota = cst[:, 256:272]
        tid = cst[:, 272:273]
        dump = cst[:, 273:274]
        blk = cst[:, 274:282]

        def f(ap):
            return ap.bitcast(F32)

        def flat(ap):
            return ap.rearrange("p k t -> p (k t)")

        def by16(ap):
            return ap.rearrange("p (e b) -> p e b", b=16)

        def wide(ap):
            return ap.unsqueeze(2).broadcast_to([P, NE, 16])

        with nc.Block() as block:
            @block.sync
            def _(eng):
                def load_x(c):
                    ev.wait(eng, "r_x2", c - 2)
                    ev.did(eng.dma_start(xr[:, c % 2, :], x[c * P:(c + 1) * P, :]), f"r_x{c % 2}", 16)

                def load(c, rows=True):
                    ev.wait(eng, "r_ol", c - 3)
                    ev.did(eng.dma_start(o[:, c % 3, :], oT[c].rearrange("d h t -> d (h t)")), f"r_o{c % 3}", 16)
                    if rows:
                        load_x(c)

                ev.did(eng.dma_start(cst[:, :], consts), "r_cst", 16)
                for i in range(4):
                    ev.did(eng.dma_start(stg[:, i, :], wo[i * P:(i + 1) * P, :]), f"r_st{i}", 16)
                load(0)
                ev.did(eng.dma_start(wc_s[:, :, :], wc.rearrange("(k p) e -> p k e", p=P)), "r_wc", 16)
                ev.did(eng.dma_start(bs[:, :], bias.rearrange("(a e) -> a e", a=1).broadcast_to([P, E2])), "r_b", 16)
                for i in range(4, NH):
                    ev.wait(eng, "r_wol", i - 4)
                    ev.did(eng.dma_start(stg[:, i % 4, :], wo[i * P:(i + 1) * P, :]), f"r_st{i % 4}", 16)
                load(1)
                load(2, False)
                for c in range(NC):
                    rows = slice(c * P, (c + 1) * P)
                    if c + 3 < NC:
                        load(c + 3, False)
                    ev.wait(eng, "r_x2", c)
                    ev.did(eng.dma_start(out[rows, :], x2[:, c % 2, :]), f"r_so{c % 2}", 16)
                    ev.wait(eng, "r_xn", c)
                    ev.did(eng.dma_start(xn2d[rows, :], xn[:, c % 2, :]), f"r_sx{c % 2}", 16)
                    if c + 2 < NC:
                        load_x(c + 2)
                for e in range(2):
                    ev.did(eng.dma_start(raw[:, e, 0:4, :], wgu[e].rearrange("(k p) f -> p k f", p=P)), f"m_wg{e}", 16)
                    ev.did(eng.dma_start(raw[:, e, 4:6, :], wd[e].rearrange("(k p) f -> p k f", p=P)), f"m_wd{e}", 16)
                ev.did(eng.dma_start(out[T:T + P, :], x2[:, 1, :]), "r_so1", 16)
                ev.wait(eng, "r_R", 3)
                for v in range(2):
                    ev.did(eng.dma_start(tbd[v].rearrange("(g p b) -> p g b", p=P, b=16), R[:, v, :, :]), "r_tw", 16)
                ev.wait(eng, "r_tw", 1, 16)
                ev.did(eng.dma_start(tb[:, :, :], tbd.rearrange("v (t s) -> t v s", s=P)), "r_tb", 16)
                ev.wait(eng, "r_tb", 0, 16)
                for b in range(2):
                    ev.wait(eng, f"r_so{b}", NC // 2 - 1 + b, 16)
                    ev.wait(eng, f"r_sx{b}", NC // 2 - 1, 16)

            @block.tensor
            def _(eng):
                def project(c):
                    ev.wait(eng, "r_x2", c - 2)
                    ev.wait(eng, "r_ol", c)
                    steps = [(o_h, wo_h), (o_h, wo_l), (o_l, wo_h)]
                    for h in range(NH):
                        if c == 0:
                            ev.wait(eng, "r_wol", h)
                        for s, (a, b) in enumerate(steps):
                            last = eng.matmul(PY[c % 2][:, :], a[:, c % 2, h * P:(h + 1) * P], b[:, h, :],
                                              start=h == 0 and s == 0, stop=h == NH - 1 and s == 2)
                    ev.did(last, "r_y")

                def turn(c):
                    ev.wait(eng, "r_cst", 0, 16)
                    ev.wait(eng, "r_xTl", c - 1)
                    ev.wait(eng, "r_xn", c)
                    for k in range(4):
                        last = eng.transpose(PX[:, k * P:(k + 1) * P], xn[:, c % 2, k * P:(k + 1) * P], ident)
                    ev.did(last, "r_xt")

                def logits(c):
                    ev.wait(eng, "r_wcl", 0)
                    ev.wait(eng, "r_xTl", c)
                    ev.wait(eng, "r_rk", c - 2)
                    ev.wait(eng, "r_e", c - 1)
                    steps = [(xT_h, wc_h), (xT_h, wc_l), (xT_l, wc_h)]
                    for s, (a, b) in enumerate(steps):
                        for k in range(4):
                            last = eng.matmul(PR[:, 0:E2], a[:, k, :], b[:, k, :],
                                              start=s == 0 and k == 0, stop=s == 2 and k == 3)
                    ev.did(last, "r_lg")

                def ranks(c):
                    ev.wait(eng, "r_e", c)
                    ev.wait(eng, "r_mb", c)
                    last = eng.matmul(PR[:, 128:128 + NE], trib[:, :], maskb[:, :], start=True, stop=c == 0)
                    if c > 0:
                        ev.wait(eng, "r_mab", c - 1)
                        last = eng.matmul(PR[:, 128:128 + NE], oneb[:, :], maccb[:, :], start=False, stop=True)
                    ev.did(last, "r_rank")

                def table(c):
                    ev.wait(eng, "r_mv", c)
                    for g in range(4):
                        cols = slice(g * P, (g + 1) * P)
                        a = OA[:, c % 2, cols]
                        eng.matmul(PB[g][:, 0:256], a, mvv[:, c % 2, 0:2, cols], start=c == 0, stop=False)
                        last = eng.matmul(PB[g][:, 128:256], a, mvv[:, c % 2, 2, cols], start=False,
                                          stop=c == NC - 1)
                    ev.did(last, "r_tbl")

                for c in range(NC + 4):
                    if c < NC:
                        project(c)
                    if 0 <= c - 1 < NC:
                        turn(c - 1)
                    if 0 <= c - 2 < NC:
                        logits(c - 2)
                    if 0 <= c - 3 < NC:
                        ranks(c - 3)
                    if 0 <= c - 4 < NC:
                        table(c - 4)
                ev.wait(eng, "r_tb", 0, 16)
                ev.wait(eng, "r_xTl", NC - 1)
                for v in range(2):
                    last = eng.transpose(PX[:, 64 * v:64 * v + 64], tb[:, v, :], cst[0:64, 0:64])
                ev.did(last, "r_tt")

            @block.vector
            def _(eng):
                chain = [0]

                def then(ins):
                    ev.did(ins, "r_dve")
                    ev.wait(eng, "r_dve", chain[0])
                    chain[0] += 1

                def low(i):
                    ev.wait(eng, "r_woh", i)
                    ev.did(eng.tensor_tensor(wo_l[:, i, :], stg[:, i % 4, :], f(wo_h[:, i, :]), ALU.subtract), "r_wol")

                def o_low(c):
                    ev.wait(eng, "r_oh", c)
                    ev.did(eng.tensor_tensor(o_l[:, c % 2, :], o[:, c % 3, :], f(o_h[:, c % 2, :]), ALU.subtract), "r_ol")

                def residual(c):
                    ev.wait(eng, "r_y", c)
                    ev.wait(eng, f"r_x{c % 2}", c // 2, 16)
                    if c >= 2:
                        ev.wait(eng, f"r_so{c % 2}", c // 2 - 1, 16)
                    ev.did(eng.tensor_tensor(x2[:, c % 2, :], PY[c % 2][:, :], xr[:, c % 2, :], ALU.add), "r_x2")
                    ev.wait(eng, "r_x2", c)
                    then(eng.bn_stats(st[:, :], x2[:, c % 2, :]))
                    ev.did(eng.bn_aggr(mv[:, :], st[:, :]), "r_mvd")

                def normal(c):
                    ev.wait(eng, "r_rstd", c)
                    ev.wait(eng, "r_xt", c - 2)
                    if c >= 2:
                        ev.wait(eng, f"r_sx{c % 2}", c // 2 - 1, 16)
                    ev.did(eng.tensor_scalar(xn[:, c % 2, :], x2[:, c % 2, :], mv[:, 0:1], vr[:, 1:2],
                                             ALU.subtract, ALU.mult), "r_xn")

                def xT_low(c):
                    ev.wait(eng, "r_xTh", c)
                    ev.did(eng.tensor_tensor(flat(xT_l[:, :, :]), PX[:, :], f(flat(xT_h[:, :, :])), ALU.subtract), "r_xTl")

                def choose(c):
                    ev.wait(eng, "r_lg", c)
                    then(eng.tensor_reduce(c1[:, 0:1], PR[:, 0:E2], axis=AX, op=ALU.max))
                    ev.did(eng.tensor_scalar(c1[:, 1:2], c1[:, 0:1], -1.0, None, ALU.mult), "r_nm")
                    ev.wait(eng, "r_e", c)
                    then(eng.reciprocal(c1[:, 3:4], c1[:, 2:3]))
                    ev.wait(eng, "r_b", 0, 16)
                    then(eng.scalar_tensor_tensor(out=zz[:, :], in0=ex[:, :], scalar=c1[:, 3:4], in1=bs[:, :],
                                                  op0=ALU.mult, op1=ALU.add))
                    then(eng.max(top[:, :], zz[:, :]))
                    then(eng.match_replace(out=zr[:, :], in_to_replace=top[:, :], in_values=zz[:, :], imm_value=-3e38))
                    eng.tensor_tensor(mask[:, :], zr[:, :], zz[:, :], ALU.not_equal)
                    ev.wait(eng, "r_rank", c - 1)
                    ev.did(eng.tensor_tensor(maskb[:, :], zr[:, 0:NE], zz[:, 0:NE], ALU.not_equal), "r_mb")
                    ev.wait(eng, "r_mb", c)
                    then(eng.scalar_tensor_tensor(out=ws[:, :], in0=ex[:, :], scalar=c1[:, 3:4], in1=mask[:, :],
                                                  op0=ALU.mult, op1=ALU.mult))
                    eng.tensor_reduce(c1[:, 4:5], ws[:, :], axis=AX, op=ALU.add)
                    then(eng.tensor_reduce(c1[:, 5:6], ws[:, NE:E2], axis=AX, op=ALU.add))
                    then(eng.tensor_scalar(c1[:, 6:7], c1[:, 4:5], 1e-20, None, ALU.add))
                    then(eng.reciprocal(c1[:, 7:8], c1[:, 6:7]))
                    then(eng.tensor_scalar(c1[:, 8:9], c1[:, 7:8], 1.5, None, ALU.mult))
                    then(eng.tensor_scalar(c1[:, 9:10], c1[:, 5:6], c1[:, 8:9], 1.0, ALU.mult, ALU.add))
                    then(eng.tensor_scalar(w[:, :], ws[:, 0:NE], c1[:, 8:9], c1[:, 9:10], ALU.mult, ALU.mult))
                    ev.wait(eng, "r_mv", c - 2)
                    then(eng.tensor_copy(w_h[:, c % 2, :], w[:, :]))
                    ev.did(eng.tensor_tensor(w_l[:, c % 2, :], w[:, :], f(w_h[:, c % 2, :]), ALU.subtract), "r_wl")

                def slots(c):
                    ev.wait(eng, "r_rank", c)
                    if c == 0:
                        then(eng.tensor_copy(macc[:, :], mask[:, 0:NE]))
                    else:
                        then(eng.tensor_tensor(macc[:, :], macc[:, :], mask[:, 0:NE], ALU.add))
                    ev.did(eng.tensor_copy(maccb[:, :], macc[:, :]), "r_mab")
                    ev.did(eng.scalar_tensor_tensor(out=rk[:, :], in0=mask[:, 0:NE], scalar=-4096.0,
                                                    in1=PR[:, 128:128 + NE], op0=ALU.mult, op1=ALU.add), "r_rk")
                    ev.wait(eng, "r_rk", c)
                    then(eng.tensor_scalar(rki[:, :], rk[:, :], 4096.0, None, ALU.add))
                    eng.tensor_scalar(ra[:, :], rki[:, :], 4, None, ALU.arith_shift_right)
                    then(eng.tensor_scalar(rb[:, :], rki[:, :], 15, None, ALU.bitwise_and))
                    io = iota.unsqueeze(1).broadcast_to([P, NE, 16])
                    ev.wait(eng, "r_tbl", c - 2)
                    eng.tensor_tensor(by16(OA[:, c % 2, :]), wide(ra[:, :]), io, ALU.is_equal)
                    ev.wait(eng, "r_mv", c - 1)
                    ev.did(eng.tensor_tensor(by16(OB[:, :]), wide(rb[:, :]), io, ALU.is_equal), "r_OB")

                ev.did(eng.memset(neg[:, :], -0.5), "r_neg")
                eng.memset(oneb[:, :], 1.0)
                ev.wait(eng, "r_cst", 0, 16)
                then(eng.tensor_copy(trib[:, :], stri))
                for i in range(4):
                    low(i)
                o_low(0)
                for i in range(4, NH):
                    low(i)
                ev.wait(eng, "r_wch", 0)
                ev.did(eng.tensor_tensor(flat(wc_l[:, :, :]), flat(wc_s[:, :, :]), f(flat(wc_h[:, :, :])), ALU.subtract), "r_wcl")
                o_low(1)
                for c in range(NC + 3):
                    if c < NC:
                        residual(c)
                    if 0 <= c - 1 < NC:
                        xT_low(c - 1)
                    if c < NC:
                        normal(c)
                    if c + 2 < NC:
                        o_low(c + 2)
                    if 0 <= c - 3 < NC:
                        slots(c - 3)
                    if 0 <= c - 2 < NC:
                        choose(c - 2)
                for g in range(4):
                    ev.wait(eng, "r_tbl", NC - 1)
                    ev.wait(eng, "r_R", g - 1)
                    b4 = blk.unsqueeze(1).unsqueeze(3).broadcast_to([P, 2, 8, 16])
                    then(eng.tensor_tensor(tmp[:, :, :, :],
                                           PB[g][:, 0:256].rearrange("p (v e b) -> p v e b", v=2, b=16),
                                           b4, ALU.mult))
                    ev.did(eng.tensor_reduce(R[:, :, g, :], tmp[:, :, :, :].rearrange("p v e b -> p v b e"),
                                             axis=AX, op=ALU.add), "r_R")
                ev.wait(eng, "r_tt", 0)
                ids, wts = PX[:, 0:64], PX[:, 64:128]
                eng.tensor_copy(wt[:, :], wts)
                then(eng.tensor_scalar(id0[:, :], ids, 0.0, None, ALU.is_equal))
                then(eng.tensor_scalar(id0[:, :], id0[:, :], dump, None, ALU.mult))
                eng.tensor_scalar(gi[:, :], ids, -1.0, 0.0, ALU.add, ALU.max)
                then(eng.tensor_scalar(id1[:, :], ids, -1.0, None, ALU.add))
                then(eng.tensor_tensor(si[:, :], id0[:, :], id1[:, :], ALU.add))

            @block.scalar
            def _(eng):
                def copy(out_, in_, kind):
                    ev.did(eng.activation(out_, in_, ACT.Copy), kind)

                def high(i):
                    ev.wait(eng, f"r_st{i % 4}", i // 4, 16)
                    copy(wo_h[:, i, :], stg[:, i % 4, :], "r_woh")

                def o_high(c):
                    ev.wait(eng, "r_y", c - 2)
                    ev.wait(eng, f"r_o{c % 3}", c // 3, 16)
                    copy(o_h[:, c % 2, :], o[:, c % 3, :], "r_oh")

                for i in range(4):
                    high(i)
                o_high(0)
                for i in range(4, NH):
                    high(i)
                ev.wait(eng, "r_wc", 0, 16)
                copy(flat(wc_h[:, :, :]), flat(wc_s[:, :, :]), "r_wch")
                o_high(1)
                for c in range(NC + 2):
                    if 0 <= c - 1 < NC:
                        ev.wait(eng, "r_xt", c - 1)
                        ev.wait(eng, "r_lg", c - 2)
                        copy(flat(xT_h[:, :, :]), PX[:, :], "r_xTh")
                    if c + 2 < NC:
                        o_high(c + 2)
                    if 0 <= c - 2 < NC:
                        ev.wait(eng, "r_nm", c - 2)
                        ev.did(eng.activation(ex[:, :], PR[:, 0:E2], ACT.Exp, bias=c1[:, 1:2],
                                              accum_out=c1[:, 2:3]), "r_e")

            @block.gpsimd
            def _(eng):
                def rstd(c):
                    ev.wait(eng, "r_mvd", c)
                    ev.wait(eng, "r_neg", 0)
                    ev.did(eng.tensor_scalar_add(vr[:, 0:1], mv[:, 1:2], 1e-5), "r_ve")
                    ev.wait(eng, "r_ve", c)
                    ev.did(eng.tensor_tensor(vr[:, 1:2], vr[:, 0:1], neg[:, :], ALU.pow), "r_rstd")

                def values(c):
                    ev.wait(eng, "r_OB", c)
                    ev.wait(eng, "r_tbl", c - 2)
                    ob = by16(OB[:, :])
                    ev.did(eng.tensor_scalar(tidc[:, c:c + 1], tid, float(c * P), None, ALU.add), "r_tid")
                    ev.wait(eng, "r_tid", c)
                    eng.tensor_scalar(mvv[:, c % 2, 0, :], OB[:, :], tidc[:, c:c + 1], None, ALU.mult)
                    ev.wait(eng, "r_wl", c)
                    eng.tensor_tensor(by16(mvv[:, c % 2, 1, :]), ob, wide(f(w_h[:, c % 2, :])), ALU.mult)
                    ev.did(eng.tensor_tensor(by16(mvv[:, c % 2, 2, :]), ob, wide(w_l[:, c % 2, :]), ALU.mult), "r_mv")

                for c in range(NC + 3):
                    if c < NC:
                        rstd(c)
                    if c >= 3:
                        values(c - 3)


def experts(nc, ev, wgu, wd, xn2d, out, gi, si, wt, raw, consts):
    with ExitStack() as ctx:
        def sb(name, shape, dt=F32):
            return ctx.enter_context(nc.sbuf_tensor("m_" + name, shape, dt))

        def ps(name, n=512):
            return ctx.enter_context(nc.psum_tensor("m_" + name, [P, n], F32))

        g_h = sb("g_h", [P, 3, 4, 512], F32R)
        g_l = sb("g_l", [P, 3, 4, 512], F32R)
        d_h = sb("d_h", [P, 4, 2, 512], F32R)
        d_l = sb("d_l", [P, 4, 2, 512], F32R)
        xg = sb("xg", [P, 5, 2, D])
        xT_h = sb("xT_h", [P, 2, 2, 4, P], F32R)
        xT_l = sb("xT_l", [P, 2, 2, 4, P], F32R)
        s = sb("s", [P, 2, 256])
        a = sb("a", [P, 2, 256])
        a_h = sb("a_h", [P, 2, 256], F32R)
        a_l = sb("a_l", [P, 2, 256], F32R)
        y = sb("y", [P, 2, D])
        ident = sb("ident", [P, P])
        spare = sb("spare", [1, 16])
        PX = [ps("PX0"), ps("PX1")]
        PG = [ps("PG0"), ps("PG1")]
        PA = [ps("PA0"), ps("PA1")]
        PY = [ps("PY0"), ps("PY1")]

        def f(ap):
            return ap.bitcast(F32)

        def flat(ap):
            return ap.rearrange("p k t -> p (k t)")

        class Flags:

            def __init__(self, eng, name):
                self.eng = eng
                self.regs = [eng.alloc_register(f"{name}{i}") for i in range(5)]

            def load(self, e):
                if 0 <= e < NE:
                    self.eng.reg_load(self.regs[e % 5], si[0:1, 2 * e + 1:2 * e + 2])

            def both(self, e, half, owed):
                if not 0 <= e < NE:
                    return
                half(e, 0)
                seen = dict(ev.seen)
                with self.eng.If_lt(self.regs[e % 5], T):
                    half(e, 1)
                ev.seen = dict(seen)
                with self.eng.Else():
                    if callable(owed):
                        owed(e)
                    else:
                        if e > 0:
                            self.eng.wait_ge(ev.sem(owed), e)
                        self.eng.sem_inc(ev.sem(owed), 1)
                ev.seen = seen

        with nc.Block() as block:
            @block.sync
            def _(eng):
                ev.did(eng.dma_start(ident[:, :], consts[:, 0:128]), "m_id", 16)
                for e in range(2, NE):
                    ev.wait(eng, "m_gl", e - 2)
                    ev.did(eng.dma_start(raw[:, e % 2, 0:4, :], wgu[e].rearrange("(k p) f -> p k f", p=P)),
                           f"m_wg{e % 2}", 16)
                    ev.wait(eng, "m_dl", e - 2)
                    ev.did(eng.dma_start(raw[:, e % 2, 4:6, :], wd[e].rearrange("(k p) f -> p k f", p=P)),
                           f"m_wd{e % 2}", 16)

            @block.gpsimd
            def _(eng):
                fl = Flags(eng, "mp")

                def gather(e, t):
                    i = 2 * e + t
                    ev.wait(eng, f"m_xt{t}", e - 5)
                    ev.did(eng.indirect_dma_start(
                        xg[:, e % 5, t, :], None, xn2d[:, :],
                        bass.IndirectOffsetOnAxis(ap=gi[:, i:i + 1], axis=0)), f"m_g{t}{e % 5}", 16)

                def scatter(e, t):
                    i = 2 * e + t
                    ev.wait(eng, f"m_y{t}", e)
                    ev.wait(eng, "m_s0", e - 1 + t, 16)
                    ev.wait(eng, "m_s1", e - 1, 16)
                    ev.did(eng.indirect_dma_start(
                        out[:, :], bass.IndirectOffsetOnAxis(ap=si[:, i:i + 1], axis=0),
                        y[:, t, :], None, compute_op=ALU.add), f"m_s{t}", 16)

                def no_gather(e):
                    ev.wait(eng, "m_xt1", e - 5)
                    ev.did(eng.dma_start(xg[0:1, e % 5, 1, 0:16], consts[0:1, 0:16]), f"m_g1{e % 5}", 16)

                def no_scatter(e):
                    ev.did(eng.dma_start(spare[0:1, :], consts[0:1, 0:16]), "m_s1", 16)

                for e in range(NE + 4):
                    fl.load(e)
                    fl.both(e, gather, no_gather)
                    fl.both(e - 4, scatter, no_scatter)
                ev.wait(eng, "m_s0", NE - 1, 16)
                ev.wait(eng, "m_s1", NE - 1, 16)

            @block.tensor
            def _(eng):
                fl = Flags(eng, "mt")

                def turn(e, t):
                    ev.wait(eng, "m_id", 0, 16)
                    ev.wait(eng, f"m_g{t}{e % 5}", e // 5, 16)
                    ev.wait(eng, f"m_xTl{t}", e - 1)
                    for k in range(4):
                        last = eng.transpose(PX[t][:, k * P:(k + 1) * P], xg[:, e % 5, t, k * P:(k + 1) * P],
                                             ident[:, :])
                    ev.did(last, f"m_xt{t}")

                def up(e, t):
                    ev.wait(eng, f"m_xTl{t}", e)
                    ev.wait(eng, f"m_a{t}", e - 1)
                    ev.wait(eng, "m_gl", e)
                    steps = [(xT_h, g_h), (xT_h, g_l), (xT_l, g_h)]
                    for i, (x_, w_) in enumerate(steps):
                        for k in range(4):
                            last = eng.matmul(PG[t][:, :], x_[:, e % 2, t, k, :], w_[:, e % 3, k, :],
                                              start=i == 0 and k == 0, stop=i == 2 and k == 3)
                    ev.did(last, f"m_gu{t}")

                def turn_a(e, t):
                    ev.wait(eng, f"m_a{t}", e)
                    ev.wait(eng, f"m_al{t}", e - 1)
                    for b in range(2):
                        last = eng.transpose(PA[t][:, b * P:(b + 1) * P], a[:, t, b * P:(b + 1) * P], ident[:, :])
                    ev.did(last, f"m_at{t}")

                def down(e, t):
                    ev.wait(eng, f"m_al{t}", e)
                    ev.wait(eng, "m_dl", e)
                    ev.wait(eng, f"m_y{t}", e - 1)
                    steps = [(a_h, d_h), (a_h, d_l), (a_l, d_h)]
                    for i, (a_, w_) in enumerate(steps):
                        for b in range(2):
                            last = eng.matmul(PY[t][:, :], a_[:, t, b * P:(b + 1) * P], w_[:, e % 4, b, :],
                                              start=i == 0 and b == 0, stop=i == 2 and b == 1)
                    ev.did(last, f"m_yd{t}")

                fl.load(0)
                fl.both(0, turn, "m_xt1")
                for e in range(NE + 2):
                    fl.load(e + 1)
                    fl.both(e, up, "m_gu1")
                    fl.both(e + 1, turn, "m_xt1")
                    fl.both(e - 2, down, "m_yd1")
                    fl.both(e - 1, turn_a, "m_at1")

            @block.vector
            def _(eng):
                fl = Flags(eng, "mv")

                def w_low(e):
                    if e >= NE:
                        return
                    ev.wait(eng, "m_gh", e)
                    ev.did(eng.tensor_tensor(flat(g_l[:, e % 3]), flat(raw[:, e % 2, 0:4, :]),
                                             f(flat(g_h[:, e % 3])), ALU.subtract), "m_gl")
                    ev.wait(eng, "m_dh", e)
                    ev.did(eng.tensor_tensor(flat(d_l[:, e % 4]), flat(raw[:, e % 2, 4:6, :]),
                                             f(flat(d_h[:, e % 4])), ALU.subtract), "m_dl")

                def x_low(e, t):
                    ev.wait(eng, f"m_xTh{t}", e)
                    ev.did(eng.tensor_tensor(flat(xT_l[:, e % 2, t]), PX[t][:, :], f(flat(xT_h[:, e % 2, t])),
                                             ALU.subtract), f"m_xTl{t}")

                def act(e, t):
                    ev.wait(eng, f"m_si{t}", e)
                    ev.wait(eng, f"m_at{t}", e - 1)
                    ev.did(eng.tensor_tensor(a[:, t, :], PG[t][:, 256:512], s[:, t, :], ALU.mult), f"m_a{t}")

                def a_low(e, t):
                    ev.wait(eng, f"m_ah{t}", e)
                    ev.did(eng.tensor_tensor(a_l[:, t, :], PA[t][:, 0:256], f(a_h[:, t, :]), ALU.subtract),
                           f"m_al{t}")

                fl.load(0)
                w_low(0)
                fl.both(0, x_low, "m_xTl1")
                w_low(1)
                for e in range(NE + 1):
                    fl.load(e + 1)
                    fl.both(e, act, "m_a1")
                    fl.both(e + 1, x_low, "m_xTl1")
                    fl.both(e - 1, a_low, "m_al1")
                    w_low(e + 2)

            @block.scalar
            def _(eng):
                fl = Flags(eng, "ms")

                def copy(out_, in_, kind):
                    ev.did(eng.activation(out_, in_, ACT.Copy), kind)

                def w_high(e):
                    if e >= NE:
                        return
                    for t in range(2):
                        ev.wait(eng, f"m_gu{t}", e - 3)
                        ev.wait(eng, f"m_yd{t}", e - 4)
                    ev.wait(eng, f"m_wg{e % 2}", e // 2, 16)
                    copy(flat(g_h[:, e % 3]), flat(raw[:, e % 2, 0:4, :]), "m_gh")
                    ev.wait(eng, f"m_wd{e % 2}", e // 2, 16)
                    copy(flat(d_h[:, e % 4]), flat(raw[:, e % 2, 4:6, :]), "m_dh")

                def x_high(e, t):
                    ev.wait(eng, f"m_xt{t}", e)
                    ev.wait(eng, f"m_gu{t}", e - 2)
                    copy(flat(xT_h[:, e % 2, t]), PX[t][:, :], f"m_xTh{t}")

                def silu(e, t):
                    ev.wait(eng, f"m_gu{t}", e)
                    ev.wait(eng, f"m_a{t}", e - 1)
                    ev.did(eng.activation(s[:, t, :], PG[t][:, 0:256], ACT.Silu), f"m_si{t}")

                def a_high(e, t):
                    ev.wait(eng, f"m_at{t}", e)
                    ev.wait(eng, f"m_yd{t}", e - 1)
                    copy(a_h[:, t, :], PA[t][:, 0:256], f"m_ah{t}")

                def weigh(e, t):
                    ev.wait(eng, f"m_yd{t}", e)
                    ev.wait(eng, f"m_s{t}", e - 1, 16)
                    ev.did(eng.activation(y[:, t, :], PY[t][:, :], ACT.Copy,
                                          scale=wt[:, 2 * e + t:2 * e + t + 1]), f"m_y{t}")

                fl.load(0)
                w_high(0)
                fl.both(0, x_high, "m_xTh1")
                w_high(1)
                for e in range(NE + 2):
                    fl.load(e + 1)
                    fl.both(e, silu, "m_si1")
                    fl.both(e + 1, x_high, "m_xTh1")
                    fl.both(e - 2, weigh, "m_y1")
                    fl.both(e - 1, a_high, "m_ah1")
                    w_high(e + 2)


def build(nc, x, wq, wk, wv, wo, wc, bias, wgu, wd, tabs, ca, cr, out):
    with ExitStack() as ctx:
        ev = Events(nc, ctx)
        oT = nc.dram_tensor("oT", [NC, P, NH, P], F32).ap()
        xn2d = nc.dram_tensor("xn2d", [T, D], F32).ap()
        tbd = nc.dram_tensor("tbd", [2, 64 * P], F32).ap()
        attention(nc, ev, x, wq, wk, wv, tabs, ca, oT)
        gi = ctx.enter_context(nc.sbuf_tensor("gi", [P, 64], U32))
        si = ctx.enter_context(nc.sbuf_tensor("si", [P, 64], U32))
        wt = ctx.enter_context(nc.sbuf_tensor("wt", [P, 64], F32))
        raw = ctx.enter_context(nc.sbuf_tensor("raw", [P, 2, 6, 512], F32))
        routing(nc, ev, x, wo, wc, bias, cr, oT, xn2d, out, tbd, gi, si, wt, raw, wgu, wd)
        experts(nc, ev, wgu, wd, xn2d, out, gi, si, wt, raw, cr)
        ev.check()


def kernel(L0_attn_x, L0_attn_Wq, L0_attn_Wk, L0_attn_Wv, L0_attn_Wo, L0_ffn_w_cls, L0_ffn_bias,
           L0_ffn_w_gate_up, L0_ffn_w_down):
    import numpy as np
    import concourse.bacc as bacc
    from concourse.bass_utils import run_bass_kernel_spmd

    i = np.arange(P)
    ca = np.stack([np.eye(P), i[:, None] <= i[None, :], np.repeat((i == P - 1)[:, None], P, 1)], 1)
    cr = np.zeros((P, CW))
    cr[:, 0:128] = np.eye(P)
    cr[:, 128:256] = i[:, None] < i[None, :]
    cr[:, 256:272] = np.arange(16)[None]
    cr[:, 272] = i + 1
    cr[:, 273] = T + 1 + i
    cr[:, 274:282] = (i[:, None] // 16) == np.arange(8)[None]
    dim = 128
    freq = np.float32(1.0) / np.power(np.float32(10000.0), np.arange(0, dim, 2, dtype=np.float32) / np.float32(dim))
    ang = np.outer(np.arange(T, dtype=np.float32), freq.astype(np.float32))
    co, sn = np.cos(ang), np.sin(ang)
    tabs = np.stack([np.concatenate([co, co], -1), np.concatenate([-sn, sn], -1)], 1).reshape(NC, P, 2, dim)
    arrays = {
        "x": np.asarray(L0_attn_x).reshape(T, D),
        "wq": np.asarray(L0_attn_Wq).T,
        "wk": np.asarray(L0_attn_Wk).T,
        "wv": np.asarray(L0_attn_Wv).T,
        "wo": np.asarray(L0_attn_Wo).T,
        "wc": np.asarray(L0_ffn_w_cls).T,
        "bias": np.asarray(L0_ffn_bias),
        "wgu": np.asarray(L0_ffn_w_gate_up),
        "wd": np.asarray(L0_ffn_w_down),
        "tabs": tabs.astype(np.float32),
        "ca": ca.astype(np.float32),
        "cr": cr.astype(np.float32),
    }
    arrays = {n: np.ascontiguousarray(a) for n, a in arrays.items()}
    nc = bacc.Bacc("TRN2", target_bir_lowering=False, num_devices=1)
    args = [nc.dram_tensor("in_" + n, a.shape, F32, kind="ExternalInput").ap() for n, a in arrays.items()]
    out = nc.dram_tensor("out", [T + P, D], F32, kind="ExternalOutput").ap()
    build(nc, *args, out)
    r = run_bass_kernel_spmd(nc, [{"in_" + n: a for n, a in arrays.items()}], core_ids=[0])
    return r.results[0]["out"][:T].reshape(1, T, D)
```

```python
from contextlib import ExitStack

import concourse.bass as bass
from concourse import mybir

P = 128
D = 512
T = 2048
NC = T // P
NH = 16
KV = 4
NG = NC * KV
NE = 32
E2 = 64
CW = 282

F32 = mybir.dt.float32
F32R = mybir.dt.float32r
I32 = mybir.dt.int32
U32 = mybir.dt.uint32
ALU = mybir.AluOpType
ACT = mybir.ActivationFunctionType
AX = mybir.AxisListType.X


class Events:

    def __init__(self, nc, ctx):
        self.nc, self.ctx, self.sems, self.seen = nc, ctx, {}, {}
        self.done, self.most = {}, {}

    def sem(self, kind):
        if kind not in self.sems:
            self.sems[kind] = self.ctx.enter_context(self.nc.semaphore("e_" + kind))
        return self.sems[kind]

    def did(self, ins, kind, by=1):
        ins.then_inc(self.sem(kind), by)
        self.done[kind] = self.done.get(kind, 0) + 1

    def wait(self, eng, kind, n, by=1):
        if n < 0:
            return
        key = (id(eng), kind)
        if self.seen.get(key, -1) < n:
            self.seen[key] = n
            self.most[kind] = max(self.most.get(kind, 0), n)
            eng.wait_ge(self.sem(kind), (n + 1) * by)

    def check(self):
        short = {k: (n, self.done.get(k, 0)) for k, n in self.most.items() if n >= self.done.get(k, 0)}
        assert not short, short


def rows_of(v_h, v_l, c):
    v, i = ((v_l, 16), (v_l, 20), (v_h, 16))[c % 3]
    return v[:, i:i + 4, :].rearrange("p k (h t) -> p (k h) t", t=P)


def attention(nc, ev, x, wq, wk, wv, wo, tabs, consts, oT, w_h, w_l, v_h, v_l):
    with ExitStack() as ctx:
        def sb(name, shape, dt=F32):
            return ctx.enter_context(nc.sbuf_tensor("a_" + name, shape, dt))

        def ps(name):
            return ctx.enter_context(nc.psum_tensor("a_" + name, [P, 512], F32))

        xin = sb("xin", [P, 2, D])
        xn = sb("xn", [P, D])
        xT_h = sb("xT_h", [P, 2, 4, P], F32R)
        xT_l = sb("xT_l", [P, 2, 4, P], F32R)
        tab = sb("tab", [P, 2, 2, P])
        t1 = sb("t1", [P, 2, 512])
        t2 = sb("t2", [P, 2, 512])
        e = sb("e", [P, 2, 512])
        fK = sb("fK", [P, 512])
        fQ = sb("fQ", [P, 3, 512])
        m = sb("m", [P, 512])
        K_h = sb("K_h", [P, 512], F32R)
        K_l = sb("K_l", [P, 512], F32R)
        V_h = sb("V_h", [P, 3, 512], F32R)
        V_l = sb("V_l", [P, 3, 512], F32R)
        KT_h = sb("KT_h", [P, 2, 512], F32R)
        KT_l = sb("KT_l", [P, 2, 512], F32R)
        QT_h = sb("QT_h", [P, 2, 512], F32R)
        QT_l = sb("QT_l", [P, 2, 512], F32R)
        z = sb("z", [P, 512])
        z_h = sb("z_h", [P, 512], F32R)
        z_l = sb("z_l", [P, 512], F32R)
        A = sb("A", [P, 2, 512])
        A_h = sb("A_h", [P, 2, 512], F32R)
        A_l = sb("A_l", [P, 2, 512], F32R)
        o = sb("o", [P, 2, 512])
        S = sb("S", [P, 512])
        S_h = sb("S_h", [P, 2, 512], F32R)
        S_l = sb("S_l", [P, 2, 512], F32R)
        cst = sb("cst", [P, 3, P])
        tri_r = sb("tri_r", [P, P], F32R)
        last_r = sb("last_r", [P, P], F32R)
        st = sb("st", [P, 2, 6])
        mv = sb("mv", [P, 2, 2])
        vr = sb("vr", [P, 2, 2])
        neg = sb("neg", [P, 1])
        den = sb("den", [P, 2, 4])

        PQ = [ps("PQ0"), ps("PQ1")]
        PT = [ps("PT0"), ps("PT1")]
        PX, PS, PO, PM = ps("PX"), ps("PS"), ps("PO"), ps("PM")

        ident = cst[:, 0, :]
        tri = cst[:, 1, :]

        def f(ap):
            return ap.bitcast(F32)

        def heads(ap):
            return ap.rearrange("p (h d) -> p h d", h=4)

        def spread(ap):
            return ap.unsqueeze(1).broadcast_to([P, 4, ap.shape[-1]])

        def unit_k(c):
            return 6 * c

        def unit_v(c):
            return 6 * c + 1

        def unit_q(n):
            return 6 * (n // 4) + 2 + n % 4

        def rot_k(c):
            return 5 * c

        def rot_q(n):
            return 5 * (n // 4) + 1 + n % 4

        def plan():
            ops = []
            for n in range(NG + 5):
                c, g = divmod(n, 4)
                if g == 0 and c < NC:
                    ops += [("PK", c), ("PV", c)]
                if n < NG:
                    ops.append(("P", n))
                if 0 <= n - 5 < NG:
                    ops.append(("O", n - 5))
                if g == 0 and 1 <= c < NC:
                    ops.append(("U", c - 1))
                if g == 1 and c < NC:
                    ops += [("TK", c), ("ZC", c)]
                if 0 <= n - 3 < NG:
                    ops.append(("T", n - 3))
                if g == 2 and c + 1 < NC:
                    ops.append(("XT", c + 1))
                if 0 <= n - 4 < NG:
                    ops.append(("S", n - 4))
            return ops

        order = plan()
        turns = [op for op in order if op[0] in ("TK", "T")]
        turn = {op: j for j, op in enumerate(turns)}

        def on_pool(i):
            return i >= 11 and i % 4 == 3

        def pair(i):
            j, k = divmod(2 * i, 4)
            w = (wk, wv)[j] if j < 2 else wq[:, (j - 2) * 512:(j - 1) * 512]
            return w[k * P:(k + 2) * P, :].rearrange("(k p) f -> p k f", p=P)

        with nc.Block() as block:
            @block.sync
            def _(eng):
                def load_x(c):
                    ev.wait(eng, "xn", c - 2)
                    ev.did(eng.dma_start(xin[:, c % 2, :], x[c * P:(c + 1) * P, :]), f"x{c % 2}", 16)

                def load_tab(c):
                    if c >= 2:
                        ev.wait(eng, "pqfree", unit_q(4 * (c - 2) + 3))
                    ev.did(eng.dma_start(tab[:, c % 2, :, :], tabs[c]), f"tab{c % 2}", 16)

                def load_wo(a, b):
                    for i in range(a, b, 4):
                        ev.did(eng.dma_start(v_l[:, i:i + 4, :],
                                             wo[i * P:(i + 4) * P, :].rearrange("(k p) f -> p k f", p=P)),
                               f"r_wo{i // 4}", 16)

                def load_o(c):
                    for b in range(2):
                        ev.wait(eng, f"oT{b}", 2 * c + 1, 16)
                    ev.did(eng.dma_start(rows_of(v_h, v_l, c), oT[c]), f"r_o{c}", 16)

                load_x(0)
                ev.did(eng.dma_start(cst[:, :, :], consts), "cst", 16)
                for i in range(12):
                    ev.did(eng.dma_start(v_l[:, 2 * i:2 * i + 2, :], pair(i)), f"st{i}", 16)
                    if i == 3:
                        load_tab(0)
                load_x(1)
                load_tab(1)
                for n in range(NG + 5):
                    c, g = divmod(n, 4)
                    if g == 0 and 1 <= c < NC - 1:
                        load_tab(c + 1)
                    if g == 2 and c + 2 < NC:
                        load_x(c + 2)
                    if n >= 5:
                        i = n - 5
                        ev.wait(eng, "o", i)
                        ev.did(eng.dma_start(oT[i // 4, :, 4 * (i % 4):4 * (i % 4) + 4, :],
                                             heads(o[:, i % 2, :])), f"oT{i % 2}", 16)
                    if n == NG - 4:
                        ev.wait(eng, "pq", unit_q(n))
                        load_wo(0, 12)
                    if n == NG - 3:
                        ev.wait(eng, "pq", unit_q(n))
                        load_wo(12, 16)
                    if n in (NG - 2, NG - 1):
                        ev.wait(eng, "pq", unit_q(n))
                        load_o(n - NG + 2)
                load_o(2)
                for b in range(2):
                    ev.wait(eng, f"oT{b}", NG // 2 - 1, 16)

            @block.tensor
            def _(eng):
                def project(u, c, i):
                    ev.wait(eng, "pqfree", u - 2)
                    ev.wait(eng, "xTl", c)
                    ev.wait(eng, "wl", 4 * i + 3 - max(i - 1, 0))
                    ev.wait(eng, "wlp", i - 2)
                    bank = PQ[u % 2]
                    xh, xl = xT_h[:, c % 2], xT_l[:, c % 2]
                    last = None
                    steps = [(xh, w_h), (xh, w_l), (xl, w_h)]
                    for s, (a, w) in enumerate(steps):
                        for k in range(4):
                            last = eng.matmul(bank[:, :], a[:, k, :], w[:, 4 * i + k, :],
                                              start=s == 0 and k == 0, stop=s == 2 and k == 3)
                    ev.did(last, "pq")

                def op_PK(c):
                    project(unit_k(c), c, 0)

                def op_PV(c):
                    project(unit_v(c), c, 1)

                def op_P(n):
                    project(unit_q(n), n // 4, 2 + n % 4)

                def op_XT(c):
                    ev.wait(eng, "cst", 0, 16)
                    ev.wait(eng, "xn", c)
                    ev.wait(eng, "xTl", c - 1)
                    for k in range(4):
                        last = eng.transpose(PX[:, k * P:(k + 1) * P], xn[:, k * P:(k + 1) * P], ident)
                    ev.did(last, "xt")

                def turned(src, j):
                    ev.wait(eng, "ptfree", j - 2)
                    for k in range(4):
                        last = eng.transpose(PT[j % 2][:, k * P:(k + 1) * P], src[:, k * P:(k + 1) * P], ident)
                    ev.did(last, "pt")

                def op_TK(c):
                    ev.wait(eng, "f", rot_k(c))
                    turned(fK[:, :], turn[("TK", c)])

                def op_T(n):
                    ev.wait(eng, "fs", n)
                    turned(fQ[:, n % 3, :], turn[("T", n)])

                def op_ZC(c):
                    ev.wait(eng, "trr", 0)
                    ev.wait(eng, "Kl", c)
                    ev.wait(eng, "S", c - 1)
                    eng.matmul(PM[:, :], tri_r[:, :], K_h[:, :], start=True, stop=False)
                    last = eng.matmul(PM[:, :], tri_r[:, :], K_l[:, :], start=False, stop=c == 0)
                    if c > 0:
                        ev.wait(eng, "zl", c - 1)
                        eng.matmul(PM[:, :], last_r[:, :], z_h[:, :], start=False, stop=False)
                        last = eng.matmul(PM[:, :], last_r[:, :], z_l[:, :], start=False, stop=True)
                    ev.did(last, "zc")

                def op_S(n):
                    c, g = divmod(n, 4)
                    ev.wait(eng, "ptfree", max(turn[("T", n)], turn[("TK", c)]))
                    ev.wait(eng, "A", n - 1)
                    kh, kl = (a[:, c % 2, g * P:(g + 1) * P] for a in (KT_h, KT_l))
                    qh, ql = QT_h[:, n % 2, :], QT_l[:, n % 2, :]
                    eng.matmul(PS[:, :], kh, qh, start=True, stop=False)
                    eng.matmul(PS[:, :], kh, ql, start=False, stop=False)
                    ev.did(eng.matmul(PS[:, :], kl, qh, start=False, stop=True), "sc")

                def op_O(n):
                    c, g = divmod(n, 4)
                    ev.wait(eng, "o", n - 1)
                    cols = slice(g * P, (g + 1) * P)
                    if c > 0:
                        ev.wait(eng, "Sl", c - 1)
                        sh, sl = S_h[:, c % 2, cols], S_l[:, c % 2, cols]
                        qh, ql = QT_h[:, n % 2, :], QT_l[:, n % 2, :]
                        eng.matmul(PO[:, :], sh, qh, start=True, stop=False)
                        eng.matmul(PO[:, :], sh, ql, start=False, stop=False)
                        eng.matmul(PO[:, :], sl, qh, start=False, stop=False)
                    ev.wait(eng, "pqfree", unit_v(c))
                    ev.wait(eng, "Al", n)
                    vh, vl = V_h[:, c % 3, cols], V_l[:, c % 3, cols]
                    ah, al = A_h[:, n % 2, :], A_l[:, n % 2, :]
                    eng.matmul(PO[:, :], vh, ah, start=c == 0, stop=False)
                    eng.matmul(PO[:, :], vh, al, start=False, stop=False)
                    ev.did(eng.matmul(PO[:, :], vl, ah, start=False, stop=True), "out")

                def op_U(c):
                    ev.wait(eng, "zl", c)
                    ev.wait(eng, "z", c)
                    ev.wait(eng, "pqfree", unit_v(c))
                    for g in range(4):
                        cols = slice(g * P, (g + 1) * P)
                        steps = [(K_h, V_h), (K_h, V_l), (K_l, V_h)]
                        for s, (a, b) in enumerate(steps):
                            last = eng.matmul(PM[:, cols], a[:, cols], b[:, c % 3, cols],
                                              start=s == 0, stop=s == 2)
                    ev.did(last, "u")

                ops = {"PK": op_PK, "PV": op_PV, "P": op_P, "XT": op_XT, "TK": op_TK, "T": op_T,
                       "ZC": op_ZC, "S": op_S, "O": op_O, "U": op_U}
                op_XT(0)
                for kind, i in order:
                    ops[kind](i)

            @block.vector
            def _(eng):
                ev.did(eng.memset(neg[:, :], -0.5), "neg")
                ev.wait(eng, "cst", 0, 16)
                eng.tensor_copy(tri_r[:, :], tri)
                ev.did(eng.tensor_copy(last_r[:, :], cst[:, 2, :]), "trr")

                def stats(c):
                    ev.wait(eng, f"x{c % 2}", c // 2, 16)
                    ev.did(eng.bn_stats(st[:, c % 2, :], xin[:, c % 2, :]), "bn")
                    ev.wait(eng, "bn", c)
                    ev.wait(eng, "xn", c - 2)
                    ev.did(eng.bn_aggr(mv[:, c % 2, :], st[:, c % 2, :]), "mv")

                def normal(c):
                    ev.wait(eng, "rstd", c)
                    ev.wait(eng, "mv", c)
                    ev.wait(eng, "xt", c - 1)
                    ev.did(eng.tensor_scalar(xn[:, :], xin[:, c % 2, :], mv[:, c % 2, 0:1], vr[:, c % 2, 1:2],
                                             ALU.subtract, ALU.mult), "xn")

                def xT_low(c):
                    ev.wait(eng, "xTh", c)
                    ev.did(eng.tensor_tensor(xT_l[:, c % 2, :, :].rearrange("p k t -> p (k t)"), PX[:, :],
                                             f(xT_h[:, c % 2, :, :]).rearrange("p k t -> p (k t)"),
                                             ALU.subtract), "xTl")

                def weight_low(i):
                    if on_pool(i):
                        return
                    ev.wait(eng, "wh", i)
                    ev.did(eng.tensor_tensor(w_l[:, i, :], v_l[:, i, :], f(w_h[:, i, :]), ALU.subtract), "wl")

                def rotate(u, r, c):
                    ev.wait(eng, "pq", u)
                    ev.wait(eng, f"tab{c % 2}", c // 2, 16)
                    ev.wait(eng, "f", r - 2)
                    q = heads(PQ[u % 2][:, :])
                    a, b = heads(t1[:, r % 2, :]), heads(t2[:, r % 2, :])
                    sn = tab[:, c % 2, 1, :]
                    eng.tensor_tensor(a, q, spread(tab[:, c % 2, 0, :]), ALU.mult)
                    eng.tensor_tensor(b[:, :, 0:64], q[:, :, 64:128], spread(sn[:, 0:64]), ALU.mult)
                    ev.did(eng.tensor_tensor(b[:, :, 64:128], q[:, :, 0:64], spread(sn[:, 64:128]), ALU.mult), "pqfree")

                def feature(r, out):
                    ev.wait(eng, "e", r)
                    ev.did(eng.scalar_tensor_tensor(out=out, in0=t1[:, r % 2, :], scalar=1.0, in1=e[:, r % 2, :],
                                                    op0=ALU.add, op1=ALU.max), "f")

                def feature_k(c):
                    ev.wait(eng, "Kl", c - 1)
                    ev.wait(eng, "Kh", c - 1)
                    if c >= 1:
                        ev.wait(eng, "pt", turn[("TK", c - 1)])
                    feature(rot_k(c), fK[:, :])

                def feature_q(n):
                    if n >= 3:
                        ev.wait(eng, "pt", turn[("T", n - 3)])
                    feature(rot_q(n), fQ[:, n % 3, :])

                def v_low(c):
                    ev.wait(eng, "out", 4 * (c - 3) + 3)
                    ev.wait(eng, "u", c - 3)
                    ev.wait(eng, "Vh", c)
                    ev.did(eng.tensor_tensor(V_l[:, c % 3, :], PQ[unit_v(c) % 2][:, :], f(V_h[:, c % 3, :]),
                                             ALU.subtract), "pqfree")

                def z_low(c):
                    ev.wait(eng, "z", c)
                    ev.did(eng.tensor_tensor(z_l[:, :], PM[:, :], f(z_h[:, :]), ALU.subtract), "zl")

                def reduce(n):
                    ev.wait(eng, "m", n)
                    ev.wait(eng, "fs", n - 2)
                    d = den[:, n % 2, :]
                    ev.did(eng.tensor_reduce(d, heads(m[:, :]), axis=AX, op=ALU.add), "den")
                    ev.wait(eng, "den", n)
                    ev.did(eng.tensor_scalar_add(d, d, 1e-6), "den1")
                    ev.wait(eng, "den1", n)
                    ev.did(eng.reciprocal(d, d), "rden")

                def turn_low(j):
                    kind, i = turns[j]
                    h, l = (KT_h, KT_l) if kind == "TK" else (QT_h, QT_l)
                    if kind == "TK":
                        ev.wait(eng, "sc", 4 * (i - 2) + 3)
                    else:
                        ev.wait(eng, "out", i - 2)
                    ev.wait(eng, "th", j)
                    ev.did(eng.tensor_tensor(l[:, i % 2, :], PT[j % 2][:, :], f(h[:, i % 2, :]), ALU.subtract),
                           "ptfree")

                def masked(n):
                    ev.wait(eng, "sc", n)
                    ev.wait(eng, "Al", n - 2)
                    ev.wait(eng, "Ah", n - 2)
                    ev.did(eng.tensor_tensor(heads(A[:, n % 2, :]), heads(PS[:, :]), spread(tri), ALU.mult), "A")

                def state(c):
                    ev.wait(eng, "u", c)
                    if c == 0:
                        ins = eng.tensor_copy(S[:, :], PM[:, :])
                    else:
                        ev.wait(eng, "Sh", c - 1)
                        ev.wait(eng, "Sl", c - 1)
                        ins = eng.tensor_tensor(S[:, :], PM[:, :], S[:, :], ALU.add)
                    ev.did(ins, "S")

                stats(0)
                normal(0)
                weight_low(0)
                xT_low(0)
                for i in range(1, 12):
                    weight_low(i)
                rotate(unit_k(0), rot_k(0), 0)
                for i in range(12, 16):
                    weight_low(i)
                v_low(0)
                for i in range(16, 24):
                    weight_low(i)
                for n in range(NG + 5):
                    c, g = divmod(n, 4)
                    if g == 0 and 0 < c < NC:
                        rotate(unit_k(c), rot_k(c), c)
                        feature_q(n - 1)
                        v_low(c)
                    if n < NG:
                        rotate(unit_q(n), rot_q(n), c)
                    if g == 0 and c < NC:
                        feature_k(c)
                    if g != 0 and n - 1 < NG or n == NG:
                        feature_q(n - 1)
                    if 0 <= n - 2 < NG:
                        reduce(n - 2)
                    if g == 1 and c < NC:
                        turn_low(turn[("TK", c)])
                    if 0 <= n - 3 < NG:
                        turn_low(turn[("T", n - 3)])
                    if 0 <= n - 4 < NG:
                        masked(n - 4)
                    if g == 1 and c < NC:
                        z_low(c)
                    if g == 0 and 1 <= c < NC:
                        state(c - 1)
                    if g == 0 and c + 1 < NC:
                        stats(c + 1)
                    if g == 1 and c + 1 < NC:
                        normal(c + 1)
                    if g == 2 and c + 1 < NC:
                        xT_low(c + 1)

            @block.scalar
            def _(eng):
                def copy(out, in_, kind):
                    ev.did(eng.activation(out, in_, ACT.Copy), kind)

                def weight_high(i):
                    ev.wait(eng, f"st{i // 2}", 0, 16)
                    copy(w_h[:, i, :], v_l[:, i, :], "wh")

                def xT_high(c):
                    ev.wait(eng, "xt", c)
                    if c >= 2:
                        ev.wait(eng, "pq", unit_q(4 * (c - 2) + 3))
                    copy(xT_h[:, c % 2, :, :].rearrange("p k t -> p (k t)"), PX[:, :], "xTh")

                def exps(r):
                    ev.wait(eng, "xr", r)
                    ev.did(eng.activation(t2[:, r % 2, :], t1[:, r % 2, :], ACT.Relu, scale=-1.0), "r")
                    ev.wait(eng, "r", r)
                    ev.did(eng.activation(e[:, r % 2, :], t2[:, r % 2, :], ACT.Exp, scale=-1.0), "e")

                def v_high(c):
                    ev.wait(eng, "pq", unit_v(c))
                    ev.wait(eng, "out", 4 * (c - 3) + 3)
                    ev.wait(eng, "u", c - 3)
                    copy(V_h[:, c % 3, :], PQ[unit_v(c) % 2][:, :], "Vh")

                def k_high(c):
                    ev.wait(eng, "f", rot_k(c))
                    ev.wait(eng, "u", c - 1)
                    ev.wait(eng, "zc", c - 1)
                    copy(K_h[:, :], fK[:, :], "Kh")

                def z_high(c):
                    ev.wait(eng, "zc", c)
                    copy(z_h[:, :], PM[:, :], "zh")
                    ev.wait(eng, "m", 4 * (c - 1) + 3)
                    copy(z[:, :], PM[:, :], "z")

                def turn_high(j):
                    kind, i = turns[j]
                    h = KT_h if kind == "TK" else QT_h
                    ev.wait(eng, "pt", j)
                    if kind == "TK":
                        ev.wait(eng, "sc", 4 * (i - 2) + 3)
                    else:
                        ev.wait(eng, "out", i - 2)
                    copy(h[:, i % 2, :], PT[j % 2][:, :], "th")

                def a_high(n):
                    ev.wait(eng, "A", n)
                    ev.wait(eng, "out", n - 2)
                    copy(A_h[:, n % 2, :], A[:, n % 2, :], "Ah")

                def s_high(c):
                    ev.wait(eng, "S", c)
                    ev.wait(eng, "out", 4 * (c - 1) + 3)
                    copy(S_h[:, (c + 1) % 2, :], S[:, :], "Sh")

                def out(n):
                    ev.wait(eng, "out", n)
                    if n >= 2:
                        ev.wait(eng, f"oT{n % 2}", n // 2 - 1, 16)
                    copy(o[:, n % 2, :], PO[:, :], "o")

                weight_high(0)
                xT_high(0)
                for i in range(1, 20):
                    weight_high(i)
                v_high(0)
                for i in range(20, 24):
                    weight_high(i)
                for n in range(NG + 5):
                    c, g = divmod(n, 4)
                    if 0 <= n - 1 < NG:
                        exps(rot_q(n - 1))
                    if g == 0 and c < NC:
                        if c > 0:
                            v_high(c)
                        exps(rot_k(c))
                    if 0 <= n - 5 < NG:
                        out(n - 5)
                    if g == 0 and c < NC:
                        k_high(c)
                    if g == 1 and c < NC:
                        turn_high(turn[("TK", c)])
                    if 0 <= n - 3 < NG:
                        turn_high(turn[("T", n - 3)])
                    if g == 1 and c < NC:
                        z_high(c)
                    if g == 2 and c + 1 < NC:
                        xT_high(c + 1)
                    if 0 <= n - 4 < NG:
                        a_high(n - 4)
                    if g == 0 and 1 <= c < NC:
                        s_high(c - 1)

            @block.gpsimd
            def _(eng):
                def rstd(c):
                    ev.wait(eng, "mv", c)
                    ev.wait(eng, "neg", 0)
                    ev.wait(eng, "xn", c - 2)
                    ev.did(eng.tensor_scalar_add(vr[:, c % 2, 0:1], mv[:, c % 2, 1:2], 1e-5), "ve")
                    ev.wait(eng, "ve", c)
                    ev.did(eng.tensor_tensor(vr[:, c % 2, 1:2], vr[:, c % 2, 0:1], neg[:, :], ALU.pow), "rstd")

                def weight_low(i):
                    ev.wait(eng, "wh", i)
                    ev.did(eng.tensor_tensor(w_l[:, i, :], v_l[:, i, :], f(w_h[:, i, :]), ALU.subtract), "wlp")

                def add(r):
                    c, i = divmod(r, 5)
                    ev.wait(eng, "pqfree", 6 * c + (0 if i == 0 else i + 1))
                    ev.did(eng.tensor_tensor(t1[:, r % 2, :], t1[:, r % 2, :], t2[:, r % 2, :], ALU.add), "xr")

                def k_low(c):
                    ev.wait(eng, "Kh", c)
                    ev.did(eng.tensor_tensor(K_l[:, :], fK[:, :], f(K_h[:, :]), ALU.subtract), "Kl")

                def s_low(c):
                    ev.wait(eng, "Sh", c)
                    ev.did(eng.tensor_tensor(S_l[:, (c + 1) % 2, :], S[:, :], f(S_h[:, (c + 1) % 2, :]),
                                             ALU.subtract), "Sl")

                def times_z(n):
                    ev.wait(eng, "f", rot_q(n))
                    ev.wait(eng, "z", n // 4)
                    ev.wait(eng, "den", n - 1)
                    g = n % 4
                    ev.did(eng.tensor_tensor(heads(m[:, :]), heads(fQ[:, n % 3, :]),
                                             spread(z[:, g * P:(g + 1) * P]), ALU.mult), "m")

                def scale(n):
                    ev.wait(eng, "rden", n)
                    q = heads(fQ[:, n % 3, :])
                    ev.did(eng.tensor_tensor(q, q, den[:, n % 2, :].unsqueeze(2).broadcast_to([P, 4, P]),
                                             ALU.mult), "fs")

                def a_low(n):
                    ev.wait(eng, "Ah", n)
                    ev.wait(eng, "out", n - 2)
                    ev.did(eng.tensor_tensor(A_l[:, n % 2, :], A[:, n % 2, :], f(A_h[:, n % 2, :]),
                                             ALU.subtract), "Al")

                rstd(0)
                for i in range(11, 16, 4):
                    weight_low(i)
                add(rot_k(0))
                for i in range(19, 24, 4):
                    weight_low(i)
                for n in range(NG + 5):
                    c, g = divmod(n, 4)
                    if 0 <= n - 2 < NG:
                        times_z(n - 2)
                    if g == 0 and 0 < c < NC:
                        add(rot_k(c))
                    if n < NG:
                        add(rot_q(n))
                    if g == 0 and c < NC:
                        k_low(c)
                    if 0 <= n - 2 < NG:
                        scale(n - 2)
                    if 0 <= n - 4 < NG:
                        a_low(n - 4)
                    if g == 0 and 1 <= c < NC:
                        s_low(c - 1)
                    if g == 0 and c + 1 < NC:
                        rstd(c + 1)


def routing(nc, ev, x, wo, wc, bias, consts, oT, xn2d, out, tbd, gi, si, wt, raw, wgu, wd, w_h_, w_l_, v_h, v_l):
    with ExitStack() as ctx:
        def sb(name, shape, dt=F32):
            return ctx.enter_context(nc.sbuf_tensor("r_" + name, shape, dt))

        def ps(name):
            return ctx.enter_context(nc.psum_tensor("r_" + name, [P, 512], F32))

        BF = mybir.dt.bfloat16
        wo_h, wo_l = w_h_, w_l_
        wc_s = sb("wc_s", [P, 4, E2])
        wc_h = sb("wc_h", [P, 4, E2], F32R)
        wc_l = sb("wc_l", [P, 4, E2], F32R)
        bs = sb("bs", [P, E2])
        cst = sb("cst", [P, CW])
        o_h = sb("o_h", [P, 2, NH * P], F32R)
        o_l = sb("o_l", [P, 2, NH * P], F32R)
        xr = sb("xr", [P, 2, D])
        x2 = sb("x2", [P, 2, D])
        xn = sb("xn", [P, 2, D])
        xT_h = sb("xT_h", [P, 4, P], F32R)
        xT_l = sb("xT_l", [P, 4, P], F32R)
        st = sb("st", [P, 6])
        mv = sb("mv", [P, 2])
        vr = sb("vr", [P, 2])
        neg = sb("neg", [P, 1])
        c1 = sb("c1", [P, 16])
        ex = sb("ex", [P, E2])
        zz = sb("zz", [P, E2])
        top = sb("top", [P, 8])
        zr = sb("zr", [P, E2])
        mask = sb("mask", [P, E2])
        maskb = sb("maskb", [P, NE], BF)
        macc = sb("macc", [P, NE])
        maccb = sb("maccb", [P, NE], BF)
        trib = sb("trib", [P, P], BF)
        oneb = sb("oneb", [P, P], BF)
        ws = sb("ws", [P, E2])
        w = sb("w", [P, NE])
        w_h = sb("w_h", [P, 2, NE], F32R)
        w_l = sb("w_l", [P, 2, NE])
        rk = sb("rk", [P, NE])
        rki = sb("rki", [P, NE], I32)
        ra = sb("ra", [P, NE], I32)
        rb = sb("rb", [P, NE], I32)
        OA = sb("OA", [P, 2, 512], F32R)
        OB = sb("OB", [P, 512])
        mvv = sb("mvv", [P, 2, 3, 512], F32R)
        tmp = sb("tmp", [P, 2, 8, 16])
        R = sb("R", [P, 2, 4, 16])
        tb = sb("tb", [64, 2, P])
        id0 = sb("id0", [P, 64])
        id1 = sb("id1", [P, 64])
        tidc = sb("tidc", [P, NC])

        PY = [ps("PY0"), ps("PY1")]
        PX, PR = ps("PX"), ps("PR")
        PB = [ps(f"PB{g}") for g in range(4)]

        ident = cst[:, 0:128]
        stri = cst[:, 128:256]
        iota = cst[:, 256:272]
        tid = cst[:, 272:273]
        dump = cst[:, 273:274]
        blk = cst[:, 274:282]

        def f(ap):
            return ap.bitcast(F32)

        def flat(ap):
            return ap.rearrange("p k t -> p (k t)")

        def heads(ap):
            return ap.rearrange("p (h t) -> p h t", t=P)

        def by16(ap):
            return ap.rearrange("p (e b) -> p e b", b=16)

        def wide(ap):
            return ap.unsqueeze(2).broadcast_to([P, NE, 16])

        with nc.Block() as block:
            @block.sync
            def _(eng):
                def load_x(c):
                    ev.wait(eng, "r_x2", c - 2)
                    ev.did(eng.dma_start(xr[:, c % 2, :], x[c * P:(c + 1) * P, :]), f"r_x{c % 2}", 16)

                def load(c):
                    ev.wait(eng, "r_ol", c - 3)
                    ev.did(eng.dma_start(rows_of(v_h, v_l, c), oT[c]), f"r_o{c % 3}", 16)

                ev.did(eng.dma_start(cst[:, :], consts), "r_cst", 16)
                ev.did(eng.dma_start(wc_s[:, :, :], wc.rearrange("(k p) e -> p k e", p=P)), "r_wc", 16)
                ev.did(eng.dma_start(bs[:, :], bias.rearrange("(a e) -> a e", a=1).broadcast_to([P, E2])), "r_b", 16)
                load_x(0)
                load_x(1)
                for c in range(NC):
                    rows = slice(c * P, (c + 1) * P)
                    if c + 3 < NC:
                        load(c + 3)
                    ev.wait(eng, "r_x2", c)
                    ev.did(eng.dma_start(out[rows, :], x2[:, c % 2, :]), f"r_so{c % 2}", 16)
                    ev.wait(eng, "r_xn", c)
                    ev.did(eng.dma_start(xn2d[rows, :], xn[:, c % 2, :]), f"r_sx{c % 2}", 16)
                    if c + 2 < NC:
                        load_x(c + 2)
                for e in range(2):
                    ev.did(eng.dma_start(raw[:, e, 0:4, :], wgu[e].rearrange("(k p) f -> p k f", p=P)), f"m_wg{e}", 16)
                    ev.did(eng.dma_start(raw[:, e, 4:6, :], wd[e].rearrange("(k p) f -> p k f", p=P)), f"m_wd{e}", 16)
                ev.did(eng.dma_start(out[T:T + P, :], x2[:, 1, :]), "r_so1", 16)
                ev.wait(eng, "r_R", 3)
                for v in range(2):
                    ev.did(eng.dma_start(tbd[v].rearrange("(g p b) -> p g b", p=P, b=16), R[:, v, :, :]), "r_tw", 16)
                ev.wait(eng, "r_tw", 1, 16)
                ev.did(eng.dma_start(tb[:, :, :], tbd.rearrange("v (t s) -> t v s", s=P)), "r_tb", 16)
                ev.wait(eng, "r_tb", 0, 16)
                for b in range(2):
                    ev.wait(eng, f"r_so{b}", NC // 2 - 1 + b, 16)
                    ev.wait(eng, f"r_sx{b}", NC // 2 - 1, 16)

            @block.tensor
            def _(eng):
                def project(c):
                    ev.wait(eng, "r_x2", c - 2)
                    ev.wait(eng, "r_ol", c)
                    steps = [(o_h, wo_h), (o_h, wo_l), (o_l, wo_h)]
                    for h in range(NH):
                        if c == 0:
                            ev.wait(eng, "r_wol", h)
                        for s, (a, b) in enumerate(steps):
                            last = eng.matmul(PY[c % 2][:, :], a[:, c % 2, h * P:(h + 1) * P], b[:, h, :],
                                              start=h == 0 and s == 0, stop=h == NH - 1 and s == 2)
                    ev.did(last, "r_y")

                def turn(c):
                    ev.wait(eng, "r_cst", 0, 16)
                    ev.wait(eng, "r_xTl", c - 1)
                    ev.wait(eng, "r_xn", c)
                    for k in range(4):
                        last = eng.transpose(PX[:, k * P:(k + 1) * P], xn[:, c % 2, k * P:(k + 1) * P], ident)
                    ev.did(last, "r_xt")

                def logits(c):
                    ev.wait(eng, "r_wcl", 0)
                    ev.wait(eng, "r_xTl", c)
                    ev.wait(eng, "r_rk", c - 2)
                    ev.wait(eng, "r_e", c - 1)
                    steps = [(xT_h, wc_h), (xT_h, wc_l), (xT_l, wc_h)]
                    for s, (a, b) in enumerate(steps):
                        for k in range(4):
                            last = eng.matmul(PR[:, 0:E2], a[:, k, :], b[:, k, :],
                                              start=s == 0 and k == 0, stop=s == 2 and k == 3)
                    ev.did(last, "r_lg")

                def ranks(c):
                    ev.wait(eng, "r_e", c)
                    ev.wait(eng, "r_mb", c)
                    last = eng.matmul(PR[:, 128:128 + NE], trib[:, :], maskb[:, :], start=True, stop=c == 0)
                    if c > 0:
                        ev.wait(eng, "r_mab", c - 1)
                        last = eng.matmul(PR[:, 128:128 + NE], oneb[:, :], maccb[:, :], start=False, stop=True)
                    ev.did(last, "r_rank")

                def table(c):
                    ev.wait(eng, "r_mv", c)
                    for g in range(4):
                        cols = slice(g * P, (g + 1) * P)
                        a = OA[:, c % 2, cols]
                        eng.matmul(PB[g][:, 0:256], a, mvv[:, c % 2, 0:2, cols], start=c == 0, stop=False)
                        last = eng.matmul(PB[g][:, 128:256], a, mvv[:, c % 2, 2, cols], start=False,
                                          stop=c == NC - 1)
                    ev.did(last, "r_tbl")

                for c in range(NC + 4):
                    if c < NC:
                        project(c)
                    if 0 <= c - 1 < NC:
                        turn(c - 1)
                    if 0 <= c - 2 < NC:
                        logits(c - 2)
                    if 0 <= c - 3 < NC:
                        ranks(c - 3)
                    if 0 <= c - 4 < NC:
                        table(c - 4)
                ev.wait(eng, "r_tb", 0, 16)
                ev.wait(eng, "r_xTl", NC - 1)
                for v in range(2):
                    last = eng.transpose(PX[:, 64 * v:64 * v + 64], tb[:, v, :], cst[0:64, 0:64])
                ev.did(last, "r_tt")

            @block.vector
            def _(eng):
                chain = [0]

                def then(ins):
                    ev.did(ins, "r_dve")
                    ev.wait(eng, "r_dve", chain[0])
                    chain[0] += 1

                def low(i):
                    ev.wait(eng, "r_woh", i)
                    ev.did(eng.tensor_tensor(wo_l[:, i, :], v_l[:, i, :], f(wo_h[:, i, :]), ALU.subtract), "r_wol")

                def o_low(c):
                    ev.wait(eng, "r_oh", c)
                    ev.did(eng.tensor_tensor(heads(o_l[:, c % 2, :]), rows_of(v_h, v_l, c), heads(f(o_h[:, c % 2, :])), ALU.subtract), "r_ol")

                def residual(c):
                    ev.wait(eng, "r_y", c)
                    ev.wait(eng, f"r_x{c % 2}", c // 2, 16)
                    if c >= 2:
                        ev.wait(eng, f"r_so{c % 2}", c // 2 - 1, 16)
                    ev.did(eng.tensor_tensor(x2[:, c % 2, :], PY[c % 2][:, :], xr[:, c % 2, :], ALU.add), "r_x2")
                    ev.wait(eng, "r_x2", c)
                    then(eng.bn_stats(st[:, :], x2[:, c % 2, :]))
                    ev.did(eng.bn_aggr(mv[:, :], st[:, :]), "r_mvd")

                def normal(c):
                    ev.wait(eng, "r_rstd", c)
                    ev.wait(eng, "r_xt", c - 2)
                    if c >= 2:
                        ev.wait(eng, f"r_sx{c % 2}", c // 2 - 1, 16)
                    ev.did(eng.tensor_scalar(xn[:, c % 2, :], x2[:, c % 2, :], mv[:, 0:1], vr[:, 1:2],
                                             ALU.subtract, ALU.mult), "r_xn")

                def xT_low(c):
                    ev.wait(eng, "r_xTh", c)
                    ev.did(eng.tensor_tensor(flat(xT_l[:, :, :]), PX[:, :], f(flat(xT_h[:, :, :])), ALU.subtract), "r_xTl")

                def choose(c):
                    ev.wait(eng, "r_lg", c)
                    then(eng.tensor_reduce(c1[:, 0:1], PR[:, 0:E2], axis=AX, op=ALU.max))
                    ev.did(eng.tensor_scalar(c1[:, 1:2], c1[:, 0:1], -1.0, None, ALU.mult), "r_nm")
                    ev.wait(eng, "r_e", c)
                    then(eng.reciprocal(c1[:, 3:4], c1[:, 2:3]))
                    ev.wait(eng, "r_b", 0, 16)
                    then(eng.scalar_tensor_tensor(out=zz[:, :], in0=ex[:, :], scalar=c1[:, 3:4], in1=bs[:, :],
                                                  op0=ALU.mult, op1=ALU.add))
                    then(eng.max(top[:, :], zz[:, :]))
                    then(eng.match_replace(out=zr[:, :], in_to_replace=top[:, :], in_values=zz[:, :], imm_value=-3e38))
                    eng.tensor_tensor(mask[:, :], zr[:, :], zz[:, :], ALU.not_equal)
                    ev.wait(eng, "r_rank", c - 1)
                    ev.did(eng.tensor_tensor(maskb[:, :], zr[:, 0:NE], zz[:, 0:NE], ALU.not_equal), "r_mb")
                    ev.wait(eng, "r_mb", c)
                    then(eng.scalar_tensor_tensor(out=ws[:, :], in0=ex[:, :], scalar=c1[:, 3:4], in1=mask[:, :],
                                                  op0=ALU.mult, op1=ALU.mult))
                    eng.tensor_reduce(c1[:, 4:5], ws[:, :], axis=AX, op=ALU.add)
                    then(eng.tensor_reduce(c1[:, 5:6], ws[:, NE:E2], axis=AX, op=ALU.add))
                    then(eng.tensor_scalar(c1[:, 6:7], c1[:, 4:5], 1e-20, None, ALU.add))
                    then(eng.reciprocal(c1[:, 7:8], c1[:, 6:7]))
                    then(eng.tensor_scalar(c1[:, 8:9], c1[:, 7:8], 1.5, None, ALU.mult))
                    then(eng.tensor_scalar(c1[:, 9:10], c1[:, 5:6], c1[:, 8:9], 1.0, ALU.mult, ALU.add))
                    then(eng.tensor_scalar(w[:, :], ws[:, 0:NE], c1[:, 8:9], c1[:, 9:10], ALU.mult, ALU.mult))
                    ev.wait(eng, "r_mv", c - 2)
                    then(eng.tensor_copy(w_h[:, c % 2, :], w[:, :]))
                    ev.did(eng.tensor_tensor(w_l[:, c % 2, :], w[:, :], f(w_h[:, c % 2, :]), ALU.subtract), "r_wl")

                def slots(c):
                    ev.wait(eng, "r_rank", c)
                    if c == 0:
                        then(eng.tensor_copy(macc[:, :], mask[:, 0:NE]))
                    else:
                        then(eng.tensor_tensor(macc[:, :], macc[:, :], mask[:, 0:NE], ALU.add))
                    ev.did(eng.tensor_copy(maccb[:, :], macc[:, :]), "r_mab")
                    ev.did(eng.scalar_tensor_tensor(out=rk[:, :], in0=mask[:, 0:NE], scalar=-4096.0,
                                                    in1=PR[:, 128:128 + NE], op0=ALU.mult, op1=ALU.add), "r_rk")
                    ev.wait(eng, "r_rk", c)
                    then(eng.tensor_scalar(rki[:, :], rk[:, :], 4096.0, None, ALU.add))
                    eng.tensor_scalar(ra[:, :], rki[:, :], 4, None, ALU.arith_shift_right)
                    then(eng.tensor_scalar(rb[:, :], rki[:, :], 15, None, ALU.bitwise_and))
                    io = iota.unsqueeze(1).broadcast_to([P, NE, 16])
                    ev.wait(eng, "r_tbl", c - 2)
                    eng.tensor_tensor(by16(OA[:, c % 2, :]), wide(ra[:, :]), io, ALU.is_equal)
                    ev.wait(eng, "r_mv", c - 1)
                    ev.did(eng.tensor_tensor(by16(OB[:, :]), wide(rb[:, :]), io, ALU.is_equal), "r_OB")

                ev.did(eng.memset(neg[:, :], -0.5), "r_neg")
                eng.memset(oneb[:, :], 1.0)
                low(0)
                low(1)
                o_low(0)
                for i in range(2, NH):
                    low(i)
                ev.wait(eng, "r_cst", 0, 16)
                then(eng.tensor_copy(trib[:, :], stri))
                ev.wait(eng, "r_wch", 0)
                ev.did(eng.tensor_tensor(flat(wc_l[:, :, :]), flat(wc_s[:, :, :]), f(flat(wc_h[:, :, :])), ALU.subtract), "r_wcl")
                o_low(1)
                for c in range(NC + 3):
                    if c < NC:
                        residual(c)
                    if 0 <= c - 1 < NC:
                        xT_low(c - 1)
                    if c < NC:
                        normal(c)
                    if c + 2 < NC:
                        o_low(c + 2)
                    if 0 <= c - 3 < NC:
                        slots(c - 3)
                    if 0 <= c - 2 < NC:
                        choose(c - 2)
                for g in range(4):
                    ev.wait(eng, "r_tbl", NC - 1)
                    ev.wait(eng, "r_R", g - 1)
                    b4 = blk.unsqueeze(1).unsqueeze(3).broadcast_to([P, 2, 8, 16])
                    then(eng.tensor_tensor(tmp[:, :, :, :],
                                           PB[g][:, 0:256].rearrange("p (v e b) -> p v e b", v=2, b=16),
                                           b4, ALU.mult))
                    ev.did(eng.tensor_reduce(R[:, :, g, :], tmp[:, :, :, :].rearrange("p v e b -> p v b e"),
                                             axis=AX, op=ALU.add), "r_R")
                for e in range(2):
                    for part in range(3):
                        split_low(ev, eng, raw, w_h_, w_l_, e, part)
                ev.wait(eng, "r_tt", 0)
                ids, wts = PX[:, 0:64], PX[:, 64:128]
                eng.tensor_copy(wt[:, :], wts)
                then(eng.tensor_scalar(id0[:, :], ids, 0.0, None, ALU.is_equal))
                then(eng.tensor_scalar(id0[:, :], id0[:, :], dump, None, ALU.mult))
                eng.tensor_scalar(gi[:, :], ids, -1.0, 0.0, ALU.add, ALU.max)
                then(eng.tensor_scalar(id1[:, :], ids, -1.0, None, ALU.add))
                then(eng.tensor_tensor(si[:, :], id0[:, :], id1[:, :], ALU.add))

            @block.scalar
            def _(eng):
                def copy(out_, in_, kind):
                    ev.did(eng.activation(out_, in_, ACT.Copy), kind)

                def high(i):
                    ev.wait(eng, f"r_wo{i // 4}", 0, 16)
                    copy(wo_h[:, i, :], v_l[:, i, :], "r_woh")

                def o_high(c):
                    ev.wait(eng, "r_y", c - 2)
                    ev.wait(eng, f"r_o{c % 3}", c // 3, 16)
                    copy(heads(o_h[:, c % 2, :]), rows_of(v_h, v_l, c), "r_oh")

                high(0)
                high(1)
                o_high(0)
                for i in range(2, NH):
                    high(i)
                ev.wait(eng, "r_wc", 0, 16)
                copy(flat(wc_h[:, :, :]), flat(wc_s[:, :, :]), "r_wch")
                o_high(1)
                for c in range(NC + 2):
                    if 0 <= c - 1 < NC:
                        ev.wait(eng, "r_xt", c - 1)
                        ev.wait(eng, "r_lg", c - 2)
                        copy(flat(xT_h[:, :, :]), PX[:, :], "r_xTh")
                    if c + 2 < NC:
                        o_high(c + 2)
                    if 0 <= c - 2 < NC:
                        ev.wait(eng, "r_nm", c - 2)
                        ev.did(eng.activation(ex[:, :], PR[:, 0:E2], ACT.Exp, bias=c1[:, 1:2],
                                              accum_out=c1[:, 2:3]), "r_e")
                ev.wait(eng, "r_y", NC - 1)
                for e in range(2):
                    for part in range(3):
                        split_high(ev, eng, raw, w_h_, e, part)

            @block.gpsimd
            def _(eng):
                def rstd(c):
                    ev.wait(eng, "r_mvd", c)
                    ev.wait(eng, "r_neg", 0)
                    ev.did(eng.tensor_scalar_add(vr[:, 0:1], mv[:, 1:2], 1e-5), "r_ve")
                    ev.wait(eng, "r_ve", c)
                    ev.did(eng.tensor_tensor(vr[:, 1:2], vr[:, 0:1], neg[:, :], ALU.pow), "r_rstd")

                def values(c):
                    ev.wait(eng, "r_OB", c)
                    ev.wait(eng, "r_tbl", c - 2)
                    ob = by16(OB[:, :])
                    ev.did(eng.tensor_scalar(tidc[:, c:c + 1], tid, float(c * P), None, ALU.add), "r_tid")
                    ev.wait(eng, "r_tid", c)
                    eng.tensor_scalar(mvv[:, c % 2, 0, :], OB[:, :], tidc[:, c:c + 1], None, ALU.mult)
                    ev.wait(eng, "r_wl", c)
                    eng.tensor_tensor(by16(mvv[:, c % 2, 1, :]), ob, wide(f(w_h[:, c % 2, :])), ALU.mult)
                    ev.did(eng.tensor_tensor(by16(mvv[:, c % 2, 2, :]), ob, wide(w_l[:, c % 2, :]), ALU.mult), "r_mv")

                for c in range(NC + 3):
                    if c < NC:
                        rstd(c)
                    if c >= 3:
                        values(c - 3)


def part_of(raw, w, e, part):
    if part < 2:
        a, b = 2 * part, 4 * (e % 3) + 2 * part
    else:
        a, b = 4, 12 + 2 * (e % 4)
    return (x[:, i:i + 2, :].rearrange("p k t -> p (k t)") for x, i in ((raw[:, e % 2], a), (w, b)))


def split_high(ev, eng, raw, w_h, e, part):
    if part != 1:
        kind = "m_wd" if part == 2 else "m_wg"
        ev.wait(eng, f"{kind}{e % 2}", e // 2, 16)
    src, high = part_of(raw, w_h, e, part)
    ev.did(eng.activation(high, src, ACT.Copy), "m_wh")


def split_low(ev, eng, raw, w_h, w_l, e, part):
    ev.wait(eng, "m_wh", 3 * e + part)
    src, high = part_of(raw, w_h, e, part)
    src, low = part_of(raw, w_l, e, part)
    ev.did(eng.tensor_tensor(low, src, high.bitcast(F32), ALU.subtract), "m_wl")


def experts(nc, ev, wgu, wd, xn2d, out, gi, si, wt, raw, consts, w_h, w_l):
    with ExitStack() as ctx:
        def sb(name, shape, dt=F32):
            return ctx.enter_context(nc.sbuf_tensor("m_" + name, shape, dt))

        def ps(name, n=512):
            return ctx.enter_context(nc.psum_tensor("m_" + name, [P, n], F32))

        xg = sb("xg", [P, 7, 2, D])
        xT_h = sb("xT_h", [P, 3, 2, 4, P], F32R)
        xT_l = sb("xT_l", [P, 3, 2, 4, P], F32R)
        s = sb("s", [P, 2, 256])
        a = sb("a", [P, 2, 2, 256])
        a_h = sb("a_h", [P, 2, 256], F32R)
        a_l = sb("a_l", [P, 2, 256], F32R)
        y = sb("y", [P, 2, 2, D])
        ident = sb("ident", [P, P])
        spare = sb("spare", [1, 16])
        PX = [ps("PX0"), ps("PX1")]
        PG = [ps("PG0"), ps("PG1")]
        PA = [ps("PA0"), ps("PA1")]
        PY = [ps("PY0"), ps("PY1")]

        def f(ap):
            return ap.bitcast(F32)

        def flat(ap):
            return ap.rearrange("p k t -> p (k t)")

        class Flags:

            def __init__(self, eng, name):
                self.eng = eng
                self.regs = [eng.alloc_register(f"{name}{i}") for i in range(7)]

            def load(self, e):
                if 0 <= e < NE:
                    self.eng.reg_load(self.regs[e % 7], si[0:1, 2 * e + 1:2 * e + 2])

            def both(self, e, half, owed):
                if not 0 <= e < NE:
                    return
                half(e, 0)
                seen = dict(ev.seen)
                with self.eng.If_lt(self.regs[e % 7], T):
                    half(e, 1)
                ev.seen = dict(seen)
                with self.eng.Else():
                    if callable(owed):
                        owed(e)
                    else:
                        if e > 0:
                            self.eng.wait_ge(ev.sem(owed), e)
                        self.eng.sem_inc(ev.sem(owed), 1)
                ev.seen = seen

        with nc.Block() as block:
            @block.sync
            def _(eng):
                ev.did(eng.dma_start(ident[:, :], consts[:, 0:128]), "m_id", 16)
                for e in range(2, NE):
                    ev.wait(eng, "m_wl", 3 * (e - 2) + 1)
                    ev.did(eng.dma_start(raw[:, e % 2, 0:4, :], wgu[e].rearrange("(k p) f -> p k f", p=P)),
                           f"m_wg{e % 2}", 16)
                    ev.wait(eng, "m_wl", 3 * (e - 2) + 2)
                    ev.did(eng.dma_start(raw[:, e % 2, 4:6, :], wd[e].rearrange("(k p) f -> p k f", p=P)),
                           f"m_wd{e % 2}", 16)

            @block.gpsimd
            def _(eng):
                fl = Flags(eng, "mp")

                def gather(e, t):
                    i = 2 * e + t
                    ev.wait(eng, f"m_xt{t}", e - 7)
                    ev.did(eng.indirect_dma_start(
                        xg[:, e % 7, t, :], None, xn2d[:, :],
                        bass.IndirectOffsetOnAxis(ap=gi[:, i:i + 1], axis=0)), f"m_g{t}{e % 7}", 16)

                def scatter(e, t):
                    i = 2 * e + t
                    ev.wait(eng, f"m_y{t}", e)
                    ev.wait(eng, "m_s0", e - 1 + t, 16)
                    ev.wait(eng, "m_s1", e - 1, 16)
                    ev.did(eng.indirect_dma_start(
                        out[:, :], bass.IndirectOffsetOnAxis(ap=si[:, i:i + 1], axis=0),
                        y[:, e % 2, t, :], None, compute_op=ALU.add), f"m_s{t}", 16)

                def no_gather(e):
                    ev.wait(eng, "m_xt1", e - 7)
                    ev.did(eng.dma_start(xg[0:1, e % 7, 1, 0:16], consts[0:1, 0:16]), f"m_g1{e % 7}", 16)

                def no_scatter(e):
                    ev.did(eng.dma_start(spare[0:1, :], consts[0:1, 0:16]), "m_s1", 16)

                for e in range(NE + 6):
                    fl.load(e)
                    fl.both(e, gather, no_gather)
                    fl.both(e - 6, scatter, no_scatter)
                ev.wait(eng, "m_s0", NE - 1, 16)
                ev.wait(eng, "m_s1", NE - 1, 16)

            @block.tensor
            def _(eng):
                fl = Flags(eng, "mt")

                def turn(e, t):
                    ev.wait(eng, "m_id", 0, 16)
                    ev.wait(eng, f"m_g{t}{e % 7}", e // 7, 16)
                    ev.wait(eng, f"m_xTl{t}", e - 1)
                    for k in range(4):
                        last = eng.transpose(PX[t][:, k * P:(k + 1) * P], xg[:, e % 7, t, k * P:(k + 1) * P],
                                             ident[:, :])
                    ev.did(last, f"m_xt{t}")

                def up(e, t):
                    ev.wait(eng, f"m_xTl{t}", e)
                    ev.wait(eng, f"m_a{t}", e - 1)
                    ev.wait(eng, "m_wl", 3 * e + 1)
                    steps = [(xT_h, w_h), (xT_h, w_l), (xT_l, w_h)]
                    for i, (x_, w_) in enumerate(steps):
                        for k in range(4):
                            last = eng.matmul(PG[t][:, :], x_[:, e % 3, t, k, :], w_[:, 4 * (e % 3) + k, :],
                                              start=i == 0 and k == 0, stop=i == 2 and k == 3)
                    ev.did(last, f"m_gu{t}")

                def turn_a(e, t):
                    ev.wait(eng, f"m_a{t}", e)
                    ev.wait(eng, f"m_al{t}", e - 1)
                    for b in range(2):
                        last = eng.transpose(PA[t][:, b * P:(b + 1) * P], a[:, e % 2, t, b * P:(b + 1) * P], ident[:, :])
                    ev.did(last, f"m_at{t}")

                def down(e, t):
                    ev.wait(eng, f"m_al{t}", e)
                    ev.wait(eng, "m_wl", 3 * e + 2)
                    ev.wait(eng, f"m_y{t}", e - 1)
                    steps = [(a_h, w_h), (a_h, w_l), (a_l, w_h)]
                    for i, (a_, w_) in enumerate(steps):
                        for b in range(2):
                            last = eng.matmul(PY[t][:, :], a_[:, t, b * P:(b + 1) * P], w_[:, 12 + 2 * (e % 4) + b, :],
                                              start=i == 0 and b == 0, stop=i == 2 and b == 1)
                    ev.did(last, f"m_yd{t}")

                for e in range(2):
                    fl.load(e)
                    fl.both(e, turn, "m_xt1")
                for e in range(NE + 2):
                    fl.load(e + 2)
                    fl.both(e, up, "m_gu1")
                    fl.both(e + 2, turn, "m_xt1")
                    fl.both(e - 2, down, "m_yd1")
                    fl.both(e - 1, turn_a, "m_at1")

            @block.vector
            def _(eng):
                fl = Flags(eng, "mv")

                def w_low(e, parts):
                    if e < NE:
                        for part in parts:
                            split_low(ev, eng, raw, w_h, w_l, e, part)

                def x_low(e, t):
                    ev.wait(eng, f"m_xTh{t}", e)
                    ev.did(eng.tensor_tensor(flat(xT_l[:, e % 3, t]), PX[t][:, :], f(flat(xT_h[:, e % 3, t])),
                                             ALU.subtract), f"m_xTl{t}")

                def act(e, t):
                    ev.wait(eng, f"m_si{t}", e)
                    ev.wait(eng, f"m_at{t}", e - 2)
                    ev.did(eng.tensor_tensor(a[:, e % 2, t, :], PG[t][:, 256:512], s[:, t, :], ALU.mult), f"m_a{t}")

                def a_low(e, t):
                    ev.wait(eng, f"m_ah{t}", e)
                    ev.did(eng.tensor_tensor(a_l[:, t, :], PA[t][:, 0:256], f(a_h[:, t, :]), ALU.subtract),
                           f"m_al{t}")

                for e in range(2):
                    fl.load(e)
                    fl.both(e, x_low, "m_xTl1")
                for e in range(NE + 1):
                    fl.load(e + 2)
                    fl.both(e, act, "m_a1")
                    fl.both(e + 2, x_low, "m_xTl1")
                    w_low(e + 2, (0,))
                    fl.both(e - 1, a_low, "m_al1")
                    w_low(e + 2, (1, 2))

            @block.scalar
            def _(eng):
                fl = Flags(eng, "ms")

                def copy(out_, in_, kind):
                    ev.did(eng.activation(out_, in_, ACT.Copy), kind)

                def w_high(e, parts):
                    if e >= NE:
                        return
                    for t in range(2):
                        ev.wait(eng, f"m_gu{t}", e - 3)
                        ev.wait(eng, f"m_yd{t}", e - 4)
                    for part in parts:
                        split_high(ev, eng, raw, w_h, e, part)

                def x_high(e, t):
                    ev.wait(eng, f"m_xt{t}", e)
                    ev.wait(eng, f"m_gu{t}", e - 3)
                    copy(flat(xT_h[:, e % 3, t]), PX[t][:, :], f"m_xTh{t}")

                def silu(e, t):
                    ev.wait(eng, f"m_gu{t}", e)
                    ev.wait(eng, f"m_a{t}", e - 1)
                    ev.did(eng.activation(s[:, t, :], PG[t][:, 0:256], ACT.Silu), f"m_si{t}")

                def a_high(e, t):
                    ev.wait(eng, f"m_at{t}", e)
                    ev.wait(eng, f"m_yd{t}", e - 1)
                    copy(a_h[:, t, :], PA[t][:, 0:256], f"m_ah{t}")

                def weigh(e, t):
                    ev.wait(eng, f"m_yd{t}", e)
                    ev.wait(eng, f"m_s{t}", e - 2, 16)
                    ev.did(eng.activation(y[:, e % 2, t, :], PY[t][:, :], ACT.Copy,
                                          scale=wt[:, 2 * e + t:2 * e + t + 1]), f"m_y{t}")

                for e in range(2):
                    fl.load(e)
                    fl.both(e, x_high, "m_xTh1")
                for e in range(NE + 2):
                    fl.load(e + 2)
                    fl.both(e, silu, "m_si1")
                    fl.both(e + 2, x_high, "m_xTh1")
                    w_high(e + 2, (0,))
                    fl.both(e - 2, weigh, "m_y1")
                    fl.both(e - 1, a_high, "m_ah1")
                    w_high(e + 2, (1, 2))


def build(nc, x, wq, wk, wv, wo, wc, bias, wgu, wd, tabs, ca, cr, out):
    with ExitStack() as ctx:
        ev = Events(nc, ctx)
        oT = nc.dram_tensor("oT", [NC, P, NH, P], F32).ap()
        xn2d = nc.dram_tensor("xn2d", [T, D], F32).ap()
        tbd = nc.dram_tensor("tbd", [2, 64 * P], F32).ap()
        with nc.sbuf_tensor("v_h", [P, 24, 512], F32) as v_h, nc.sbuf_tensor("v_l", [P, 24, 512], F32) as v_l:
            pass
        w_h = ctx.enter_context(nc.sbuf_tensor("w_h", [P, 24, 512], F32R))
        w_l = ctx.enter_context(nc.sbuf_tensor("w_l", [P, 24, 512], F32R))
        attention(nc, ev, x, wq, wk, wv, wo, tabs, ca, oT, w_h, w_l, v_h, v_l)
        gi = ctx.enter_context(nc.sbuf_tensor("gi", [P, 64], U32))
        si = ctx.enter_context(nc.sbuf_tensor("si", [P, 64], U32))
        wt = ctx.enter_context(nc.sbuf_tensor("wt", [P, 64], F32))
        raw = ctx.enter_context(nc.sbuf_tensor("raw", [P, 2, 6, 512], F32))
        routing(nc, ev, x, wo, wc, bias, cr, oT, xn2d, out, tbd, gi, si, wt, raw, wgu, wd, w_h, w_l, v_h, v_l)
        experts(nc, ev, wgu, wd, xn2d, out, gi, si, wt, raw, cr, w_h, w_l)
        ev.check()


def kernel(L0_attn_x, L0_attn_Wq, L0_attn_Wk, L0_attn_Wv, L0_attn_Wo, L0_ffn_w_cls, L0_ffn_bias,
           L0_ffn_w_gate_up, L0_ffn_w_down):
    import numpy as np
    import concourse.bacc as bacc
    from concourse.bass_utils import run_bass_kernel_spmd

    i = np.arange(P)
    ca = np.stack([np.eye(P), i[:, None] <= i[None, :], np.repeat((i == P - 1)[:, None], P, 1)], 1)
    cr = np.zeros((P, CW))
    cr[:, 0:128] = np.eye(P)
    cr[:, 128:256] = i[:, None] < i[None, :]
    cr[:, 256:272] = np.arange(16)[None]
    cr[:, 272] = i + 1
    cr[:, 273] = T + 1 + i
    cr[:, 274:282] = (i[:, None] // 16) == np.arange(8)[None]
    dim = 128
    freq = np.float32(1.0) / np.power(np.float32(10000.0), np.arange(0, dim, 2, dtype=np.float32) / np.float32(dim))
    ang = np.outer(np.arange(T, dtype=np.float32), freq.astype(np.float32))
    co, sn = np.cos(ang), np.sin(ang)
    tabs = np.stack([np.concatenate([co, co], -1), np.concatenate([-sn, sn], -1)], 1).reshape(NC, P, 2, dim)
    arrays = {
        "x": np.asarray(L0_attn_x).reshape(T, D),
        "wq": np.asarray(L0_attn_Wq).T,
        "wk": np.asarray(L0_attn_Wk).T,
        "wv": np.asarray(L0_attn_Wv).T,
        "wo": np.asarray(L0_attn_Wo).T,
        "wc": np.asarray(L0_ffn_w_cls).T,
        "bias": np.asarray(L0_ffn_bias),
        "wgu": np.asarray(L0_ffn_w_gate_up),
        "wd": np.asarray(L0_ffn_w_down),
        "tabs": tabs.astype(np.float32),
        "ca": ca.astype(np.float32),
        "cr": cr.astype(np.float32),
    }
    arrays = {n: np.ascontiguousarray(a) for n, a in arrays.items()}
    nc = bacc.Bacc("TRN2", target_bir_lowering=False, num_devices=1)
    args = [nc.dram_tensor("in_" + n, a.shape, F32, kind="ExternalInput").ap() for n, a in arrays.items()]
    out = nc.dram_tensor("out", [T + P, D], F32, kind="ExternalOutput").ap()
    build(nc, *args, out)
    r = run_bass_kernel_spmd(nc, [{"in_" + n: a for n, a in arrays.items()}], core_ids=[0])
    return r.results[0]["out"][:T].reshape(1, T, D)
```
